# Optimizing a Trainium2 kernel written in Bass

```python
import numpy as np
import jax
import jax.numpy as jnp

def _softmax(x, axis=-1):
    return jax.nn.softmax(x, axis=axis)

def _gelu(x):
    return jax.nn.gelu(x, approximate=True)

def _silu(x):
    return jax.nn.silu(x)

def _sigmoid(x):
    return jax.nn.sigmoid(x)

def _layernorm(x, axis=-1, eps=1e-05):
    m = jnp.mean(x, axis=axis, keepdims=True)
    v = jnp.var(x, axis=axis, keepdims=True)
    return (x - m) / jnp.sqrt(v + eps)

def _scatter_add(tgt, idx, src, axis=0):
    return tgt.at[idx].add(src)

def _segment_sum(src, seg, n):
    return jax.ops.segment_sum(src, seg, n)
kernel_name = 'mk_decoder_postln_d1_seqx_r8_e54a5b'

def setup_inputs(seed: int=0):
    np.random.seed(seed)
    _w = jnp.asarray

    def _rec_inputs():
        import jax
        import jax.numpy as jnp
        _rk = jax.random.key(seed)
        x = -0.0002928 + 1 * jax.random.normal(jax.random.fold_in(_rk, 1), (128, 64, 128), jnp.float32)
        _lenS = 64 - jax.random.randint(jax.random.fold_in(_rk, 7), (128,), 0, max(1, 64 // 4) + 1, jnp.int32)
        _lenS2 = 64 - jax.random.randint(jax.random.fold_in(_rk, 8), (128,), 0, max(1, 64 // 4) + 1, jnp.int32)
        _ctx_1024P = jax.random.normal(jax.random.fold_in(_rk, 11), (128, 16, 128), jnp.float32)
        _ctx_1024c = jax.random.dirichlet(jax.random.fold_in(_rk, 511), 0.3 * jnp.ones((16,), jnp.float32), (128, 64))
        _ctx_1024t = jnp.einsum('bsk,bkd->bsd', _ctx_1024c, _ctx_1024P)
        _ctx_1024t = _ctx_1024t * jax.lax.rsqrt(jnp.mean(jnp.square(_ctx_1024t)) + 1e-12) * 0.953939
        ctx_1024 = -1.39393e-06 + 0.999914 * (_ctx_1024t + 0.3 * jax.random.normal(jax.random.fold_in(_rk, 611), (128, 64, 128), jnp.float32))
        return (x, ctx_1024)
    x, ctx_1024 = _rec_inputs()

    def _L0_attn_setup():
        import jax, jax.numpy as jnp
        import numpy as np
        D_MODEL, D_STATE, D_CONV, EXPAND = (128, 16, 4, 2)
        D_INNER = EXPAND * D_MODEL
        DT_RANK = D_MODEL // 16
        BATCH, SEQLEN = (2, 128)
        key = jax.random.key(seed)
        ks = jax.random.split(key, 10)
        s = lambda k, shape, scale: jax.random.normal(k, shape, dtype=jnp.float32) * scale
        inp = {'x': s(ks[0], (BATCH, SEQLEN, D_MODEL), 1.0), 'W_in': s(ks[1], (2 * D_INNER, D_MODEL), D_MODEL ** (-0.5)), 'conv_w': s(ks[2], (D_INNER, D_CONV), D_CONV ** (-0.5)), 'conv_b': s(ks[3], (D_INNER,), 0.02), 'W_xp': s(ks[4], (DT_RANK + 2 * D_STATE, D_INNER), D_INNER ** (-0.5)), 'W_dt': s(ks[5], (D_INNER, DT_RANK), DT_RANK ** (-0.5)), 'b_dt': s(ks[6], (D_INNER,), 0.1), 'A_log': jnp.log(jnp.broadcast_to(jnp.arange(1, D_STATE + 1, dtype=jnp.float32), (D_INNER, D_STATE))), 'D': jnp.ones((D_INNER,), dtype=jnp.float32), 'W_out': s(ks[7], (D_MODEL, D_INNER), D_INNER ** (-0.5))}
        return inp
    _L0_attn_all = _L0_attn_setup()
    _L0_attn_in = {k: v for k, v in _L0_attn_all.items() if k in ('W_in', 'conv_w', 'conv_b', 'W_xp', 'W_dt', 'b_dt', 'A_log', 'D', 'W_out')}
    del _L0_attn_all

    def _L0_xattn_setup():
        import jax, jax.numpy as jnp
        import numpy as np
        B, T, D, H = (2, 256, 128, 16)
        DH = D // H
        key = jax.random.key(seed)
        ks = jax.random.split(key, 11)
        s = 1.0 / np.sqrt(D)
        return {'q': jax.random.normal(ks[0], (B, T, D), jnp.float32), 'k': jax.random.normal(ks[1], (B, T, D), jnp.float32), 'v': jax.random.normal(ks[2], (B, T, D), jnp.float32), 'wq_w': jax.random.normal(ks[3], (D, D), jnp.float32) * s, 'wq_b': jnp.zeros((D,), jnp.float32), 'wk_w': jax.random.normal(ks[4], (D, D), jnp.float32) * s, 'wk_b': jnp.zeros((D,), jnp.float32), 'wv_w': jax.random.normal(ks[5], (D, D), jnp.float32) * s, 'wv_b': jnp.zeros((D,), jnp.float32), 'wo_w': jax.random.normal(ks[6], (D, D), jnp.float32) * s, 'wo_b': jnp.zeros((D,), jnp.float32)}
    _L0_xattn_all = _L0_xattn_setup()
    _L0_xattn_in = {k: v for k, v in _L0_xattn_all.items() if k in ('wq_w', 'wq_b', 'wk_w', 'wk_b', 'wv_w', 'wv_b', 'wo_w', 'wo_b')}
    del _L0_xattn_all

    def _L0_ffn_setup():
        import jax, jax.numpy as jnp
        import numpy as np
        D_MODEL = 128
        D_HIDDEN = 512
        N_EXPERTS = 8
        TOP_K = 2
        ROUTER_TEMP = 1.0
        key = jax.random.key(seed)
        ks = jax.random.split(key, 6)
        B, S = (2, 256)
        x = jax.random.normal(ks[0], (B, S, D_MODEL), dtype=jnp.float32)
        router_w = jax.random.normal(ks[1], (N_EXPERTS, D_MODEL), dtype=jnp.float32) * 0.01
        fc1_w = jax.random.normal(ks[2], (N_EXPERTS, D_HIDDEN, D_MODEL), dtype=jnp.float32) * (1.0 / np.sqrt(D_MODEL))
        fc1_b = jax.random.normal(ks[3], (N_EXPERTS, D_HIDDEN), dtype=jnp.float32) * 0.01
        fc2_w = jax.random.normal(ks[4], (N_EXPERTS, D_MODEL, D_HIDDEN), dtype=jnp.float32) * (1.0 / np.sqrt(D_HIDDEN))
        fc2_b = jax.random.normal(ks[5], (N_EXPERTS, D_MODEL), dtype=jnp.float32) * 0.01
        return {'x': x, 'router_w': router_w, 'fc1_w': fc1_w, 'fc1_b': fc1_b, 'fc2_w': fc2_w, 'fc2_b': fc2_b}
    _L0_ffn_all = _L0_ffn_setup()
    _L0_ffn_in = {k: v for k, v in _L0_ffn_all.items() if k in ('router_w', 'fc1_w', 'fc1_b', 'fc2_w', 'fc2_b')}
    del _L0_ffn_all
    return {'x': x, 'ctx_1024': ctx_1024, 'L0_attn_W_in': _L0_attn_in['W_in'], 'L0_attn_conv_w': _L0_attn_in['conv_w'], 'L0_attn_conv_b': _L0_attn_in['conv_b'], 'L0_attn_W_xp': _L0_attn_in['W_xp'], 'L0_attn_W_dt': _L0_attn_in['W_dt'], 'L0_attn_b_dt': _L0_attn_in['b_dt'], 'L0_attn_A_log': _L0_attn_in['A_log'], 'L0_attn_D': _L0_attn_in['D'], 'L0_attn_W_out': _L0_attn_in['W_out'], 'L0_xattn_wq_w': _L0_xattn_in['wq_w'], 'L0_xattn_wq_b': _L0_xattn_in['wq_b'], 'L0_xattn_wk_w': _L0_xattn_in['wk_w'], 'L0_xattn_wk_b': _L0_xattn_in['wk_b'], 'L0_xattn_wv_w': _L0_xattn_in['wv_w'], 'L0_xattn_wv_b': _L0_xattn_in['wv_b'], 'L0_xattn_wo_w': _L0_xattn_in['wo_w'], 'L0_xattn_wo_b': _L0_xattn_in['wo_b'], 'L0_ffn_router_w': _L0_ffn_in['router_w'], 'L0_ffn_fc1_w': _L0_ffn_in['fc1_w'], 'L0_ffn_fc1_b': _L0_ffn_in['fc1_b'], 'L0_ffn_fc2_w': _L0_ffn_in['fc2_w'], 'L0_ffn_fc2_b': _L0_ffn_in['fc2_b']}

def reference(x, ctx_1024, L0_attn_W_in, L0_attn_conv_w, L0_attn_conv_b, L0_attn_W_xp, L0_attn_W_dt, L0_attn_b_dt, L0_attn_A_log, L0_attn_D, L0_attn_W_out, L0_xattn_wq_w, L0_xattn_wq_b, L0_xattn_wk_w, L0_xattn_wk_b, L0_xattn_wv_w, L0_xattn_wv_b, L0_xattn_wo_w, L0_xattn_wo_b, L0_ffn_router_w, L0_ffn_fc1_w, L0_ffn_fc1_b, L0_ffn_fc2_w, L0_ffn_fc2_b):
    import jax
    import jax.numpy as jnp

    def _L0_attn_ref(x, W_in, conv_w, conv_b, W_xp, W_dt, b_dt, A_log, D, W_out):
        import jax, jax.numpy as jnp
        import numpy as np
        D_MODEL, D_STATE, D_CONV, EXPAND = (128, 16, 4, 2)
        D_INNER = EXPAND * D_MODEL
        DT_RANK = D_MODEL // 16
        BATCH, SEQLEN = (2, 128)
        B, L, _ = x.shape
        d_conv = conv_w.shape[1]
        d_state = A_log.shape[1]
        dt_rank = W_dt.shape[1]
        xz = jnp.einsum('bld,ed->ble', x, W_in)
        x_in, z = jnp.split(xz, 2, axis=-1)
        xp = jnp.pad(x_in, ((0, 0), (d_conv - 1, 0), (0, 0)))
        x_conv = conv_b
        for k in range(d_conv):
            x_conv = x_conv + xp[:, k:k + L, :] * conv_w[:, k]
        x_conv = jax.nn.silu(x_conv)
        x_dbl = jnp.einsum('ble,fe->blf', x_conv, W_xp)
        dt_lo, Bm, Cm = jnp.split(x_dbl, [dt_rank, dt_rank + d_state], axis=-1)
        dt = jax.nn.softplus(jnp.einsum('blr,er->ble', dt_lo, W_dt) + b_dt)
        A = -jnp.exp(A_log)
        dA = jnp.exp(dt[..., None] * A)
        dBx = dt[..., None] * Bm[:, :, None, :] * x_conv[..., None]

        def step(h, inputs):
            dA_t, dBx_t, C_t = inputs
            h = dA_t * h + dBx_t
            y_t = jnp.einsum('ben,bn->be', h, C_t)
            return (h, y_t)
        h0 = jnp.zeros((B, x_in.shape[-1], d_state), x.dtype)
        _, ys = jax.lax.scan(step, h0, (dA.transpose(1, 0, 2, 3), dBx.transpose(1, 0, 2, 3), Cm.transpose(1, 0, 2)))
        y = ys.transpose(1, 0, 2) + x_conv * D
        y = y * jax.nn.silu(z)
        return jnp.einsum('ble,de->bld', y, W_out)

    def _L0_xattn_ref(q, k, v, wq_w, wq_b, wk_w, wk_b, wv_w, wv_b, wo_w, wo_b):
        import jax, jax.numpy as jnp
        import numpy as np
        B, T, D, H = (2, 256, 128, 16)
        DH = D // H
        b, t, d = q.shape
        wq = (q @ wq_w.T + wq_b).reshape(b, t, H, DH)
        wk = (k @ wk_w.T + wk_b).reshape(b, t, H, DH)
        wv = (v @ wv_w.T + wv_b).reshape(b, t, H, DH)
        scores = jnp.einsum('bthd,bshd->bhts', wq, wk) / jnp.sqrt(jnp.float32(DH))
        probs = jax.nn.softmax(scores, axis=-1)
        attn = jnp.einsum('bhts,bshd->bthd', probs, wv)
        attn = attn.reshape(b, t, d)
        return attn @ wo_w.T + wo_b

    def _L0_ffn_ref(x, router_w, fc1_w, fc1_b, fc2_w, fc2_b):
        import jax, jax.numpy as jnp
        import numpy as np
        D_MODEL = 128
        D_HIDDEN = 512
        N_EXPERTS = 8
        TOP_K = 2
        ROUTER_TEMP = 1.0
        B, S, D = x.shape
        T = B * S
        flat = x.reshape(T, D)
        logits = flat @ router_w.T / ROUTER_TEMP
        topk_vals, topk_idx = jax.lax.top_k(logits, TOP_K)
        routing_w = jax.nn.softmax(topk_vals, axis=-1)
        combine = jnp.zeros((T, N_EXPERTS), dtype=x.dtype)
        combine = combine.at[jnp.arange(T)[:, None], topk_idx].add(routing_w)
        h = jnp.einsum('td,ehd->eth', flat, fc1_w) + fc1_b[:, None, :]
        h = jax.nn.gelu(h, approximate=True)
        y = jnp.einsum('eth,eoh->eto', h, fc2_w) + fc2_b[:, None, :]
        out = jnp.einsum('te,eto->to', combine, y)
        return out.reshape(B, S, -1)
    x = _layernorm(x + _L0_attn_ref(x, L0_attn_W_in, L0_attn_conv_w, L0_attn_conv_b, L0_attn_W_xp, L0_attn_W_dt, L0_attn_b_dt, L0_attn_A_log, L0_attn_D, L0_attn_W_out), axis=-1)
    x = _layernorm(x + _L0_xattn_ref(x, ctx_1024, ctx_1024, L0_xattn_wq_w, L0_xattn_wq_b, L0_xattn_wk_w, L0_xattn_wk_b, L0_xattn_wv_w, L0_xattn_wv_b, L0_xattn_wo_w, L0_xattn_wo_b), axis=-1)
    x = _layernorm(x + _L0_ffn_ref(x, L0_ffn_router_w, L0_ffn_fc1_w, L0_ffn_fc1_b, L0_ffn_fc2_w, L0_ffn_fc2_b), axis=-1)
    return x

_drawn_inputs = setup_inputs


def setup_inputs(seed=0):
    import zlib

    import numpy as np

    out = dict(_drawn_inputs(seed))
    spreads = {'L0_attn_D': (1.0, 0.2),
     'L0_xattn_wq_b': (0.0, 0.1),
     'L0_xattn_wk_b': (0.0, 0.8),
     'L0_xattn_wv_b': (0.0, 0.1),
     'L0_xattn_wo_b': (0.0, 0.1)}
    factors = {'L0_ffn_fc1_b': 8.0, 'L0_ffn_fc2_b': 8.0}
    for name, (base, spread) in spreads.items():
        noise = np.random.default_rng([zlib.crc32(name.encode()), seed]).standard_normal(out[name].shape)
        drawn = base * np.exp(spread * noise) if base else spread * noise
        out[name] = jnp.asarray(drawn.astype(out[name].dtype))
    for name, factor in factors.items():
        out[name] = (out[name] * factor).astype(out[name].dtype)
    return out
```

```python
from contextlib import ExitStack

import concourse.bass as bass
from concourse import mybir

BATCH, SEQ, D = 128, 64, 128
E_IN, NSTATE, NCONV, DTR = 256, 16, 4, 8
HEADS, DH = 16, 8
NEXP, HID = 8, 512
P = 128
TOK = 512
CHUNKS = BATCH * SEQ // TOK
NB = TOK // SEQ
NT = TOK // P
HALVES = E_IN // P
HB4 = HID // P
SLOTS = NSTATE
EPS = 1e-5

START = {"F": 0, "S": 1, "A": 2, "M": 3, "O": 4}

COLS = {}
_n = 0
for _name, _w in [("conv_w", HALVES * NCONV), ("conv_b", HALVES), ("b_dt", HALVES), ("skip_d", HALVES),
                  ("a_log", HALVES * NSTATE), ("bq", 1), ("bk", 1), ("bv", 1), ("b1", NEXP * HB4),
                  ("router", NEXP), ("group_mask", 4), ("head_mask", 4), ("half_mask", 2),
                  ("ident", P), ("w_dt_rows", E_IN), ("select", 32),
                  ("tie_order", NEXP), ("w_xp", HALVES * 104), ("w_in", 2 * E_IN), ("w_out", HALVES * D),
                  ("wq", D), ("wk", D), ("wv", D), ("wo", D)]:
    COLS[_name] = (_n, _n + _w)
    _n += _w
NCOLS = _n
COLS["b2_rows"] = (COLS["w_dt_rows"][0], COLS["w_dt_rows"][0] + D)
COLS["bo_row"] = (COLS["w_dt_rows"][0] + D, COLS["w_dt_rows"][0] + 2 * D)

DECAY_SLOTS = {0: [0, 1, 2], 2: [3, 4], 3: [5, 6], 6: [7, 8], 7: [9, 10], 10: [11, 12], 11: [13, 14], 14: [15]}
GROUP = 4
NGROUP = NSTATE // GROUP
UNITS = NSTATE * HALVES
DECAY_RING, SCAN_RING, PROD_RING = 8, 4, 4
HID_UNITS = NEXP * HB4
HID_RING = 8
C_USES = NSTATE + HALVES


def c_use(n):
    return n if n < 4 else n + HALVES


def z_use(h):
    return 4 + h


A_ORDER = (["k", "v0", "v1", "out", "x1t", "q0", "sc00", "sc01", "sc10", "sc11", "q1", "pt00", "pt01",
            "pv0", "pt10", "pt11", "sc20", "sc21", "pv1", "sc30", "sc31", "pt20", "pt21", "pv2",
            "pt30", "pt31", "pv3", "att", "o"])
NA = len(A_ORDER)
Y_ORDER = ["x2t", "router", "e0", "e1", "comb", "b2", "e2", "e3", "e4", "e5", "e6", "e7"]
NY = len(Y_ORDER)
NF = 5


def decoder_layer(nc, x_t, x_tok, ctx_t, params, w1, w2, out):
    F32, BF16 = mybir.dt.float32, mybir.dt.bfloat16
    ALU, ACT, AX = mybir.AluOpType, mybir.ActivationFunctionType, mybir.AxisListType

    ctx = ExitStack()
    with ctx:
        def sb(name, shape, dt=F32):
            return ctx.enter_context(nc.sbuf_tensor(name, shape, dt))

        def pb(name):
            return ctx.enter_context(nc.psum_tensor(name, [P, TOK], F32))

        def sem(name):
            return ctx.enter_context(nc.semaphore(name))

        par = sb("par", [P, NCOLS])
        w1s = sb("w1s", [P, HID_UNITS * P])
        w2s = sb("w2s", [P, HID_UNITS * D])
        select_bf = sb("select_bf", [96, 32], BF16)
        neg_a = sb("neg_a", [P, HALVES * NSTATE])
        qscale = sb("qscale", [P, 8])
        kbias = sb("kbias", [P, 4])
        bo = sb("bo", [P, D])
        half_pow = sb("half_pow", [P, NT])
        xt = sb("xt", [P, 2, TOK])
        dt = sb("dt", [P, 2, HALVES, TOK])
        du = sb("du", [P, 2, HALVES, TOK])
        xc = sb("xc", [P, 2, HALVES, TOK])
        bc3 = sb("bc3", [96, 2, TOK], BF16)
        low = sb("low", [P, TOK])
        dt_low, comb_t = low[96:96 + DTR, :], low[0:NEXP, :]
        gz = sb("gz", [P, HALVES, TOK])
        decay = sb("decay", [P, DECAY_RING, TOK])
        state = sb("state", [P, SCAN_RING, TOK])
        c_all = sb("c_all", [P, 2, TOK])
        prod = sb("prod", [P, PROD_RING, 1 + GROUP, TOK])
        xtok = sb("xtok", [P, NT, D])
        ctxs = sb("ctxs", [P, TOK])
        x1 = sb("x1", [P, NT, D])
        x1t = sb("x1t", [P, TOK])
        qm = sb("qm", [P, 4, TOK // 2])
        km = sb("km", [P, 4, TOK])
        vv = sb("vv", [P, NB * 8, 2 * (DH + 1)])
        probs = sb("probs", [P, 2, HEADS * SEQ])
        probs_t = sb("probs_t", [P, 8, P])
        att = sb("att", [P, NT, D])
        mx = sb("mx", [P, 2, 8])
        rden = sb("rden", [P, HEADS])
        x2 = sb("x2", [P, NT, D])
        ln_st = sb("ln_st", [P, 3, NT, 6])
        ln_mean = sb("ln_mean", [P, 3, NT])
        ln_tmp = sb("ln_tmp", [P, 2, NT])
        ln_ve = sb("ln_ve", [P, 3, NT])
        ln_rs = sb("ln_rs", [P, 3, NT])
        x2t = sb("x2t", [P, TOK])
        hid = sb("hid", [P, HID_RING, TOK])
        acc = sb("acc", [P, NT, D])
        obuf = att
        rl = sb("rl", [P, 4, NT, NEXP])
        rm = sb("rm", [P, 6, NT])
        comb = sb("comb", [P, NT, NEXP])
        ones_row = x2t[0:1, 0:P]

        def pc(name, a=0, b=None, rows=P, row0=0):
            lo, hi = COLS[name]
            return par[row0:row0 + rows, lo + a:(hi if b is None else lo + b)]

        ident = pc("ident")

        b_ps, c_ps, f_ps, y_ps = pb("b_ps"), pb("c_ps"), pb("f_ps"), pb("y_ps")
        h_ps = [pb("h_ps0"), pb("h_ps1")]
        a_ps = [pb("a_ps0"), pb("a_ps1")]

        par_in, w1_in, w2_in = sem("par_in"), sem("w1_in"), sem("w2_in")
        xt_in, ctx_in, xtok_in, stored = sem("xt_in"), sem("ctx_in"), sem("xtok_in"), sem("stored")
        setup = {n: sem("setup_" + n) for n in ("dve", "act", "pe", "pool")}
        xproj_done = sem("f_ps_filled")
        x_in_done = sem("x_in_copied")
        conv_done = sem("conv_step")
        silu_done = sem("silu_done")
        dtlow_done = sem("dt_low_copied")
        split_done = sem("bc_split_step")
        sp_parts = sem("softplus_parts")
        sp_exp = sem("softplus_exp")
        sp_ln = sem("softplus_ln")
        dt_done = sem("dt_done")
        du_done = sem("du_done")
        b_ready = sem("b_ready")
        c_ready = sem("c_ps_filled")
        c_taken = sem("c_ps_taken")
        decay_done = sem("decay_done")
        input_done = sem("scan_input_done")
        scan_done = sem("scan_done")
        prod_done = sem("prod_done")
        sum_done = sem("sum_done")
        last_sum = sem("last_sum_done")
        gate_step = sem("gate_step")
        a_filled = sem("a_ps_filled")
        k_done, v_done, x1t_done = sem("k_done"), sem("v_done"), sem("x1t_done")
        q_done = sem("q_done")
        max_done = sem("max_done")
        shift_done = sem("shift_done")
        exp_done = sem("exp_done")
        pt_done = sem("probs_t_done")
        rden_done = sem("rden_done")
        att_done = sem("att_done")
        att_t_done = sem("att_t_done")
        ln_step = [sem(f"ln{i + 1}_step") for i in range(3)]
        ln_rstd = [sem(f"ln{i + 1}_rstd") for i in range(3)]
        ln_out = [sem(f"ln{i + 1}_out") for i in range(3)]
        x1_biased = sem("x1_biased")
        x2t_done = sem("x2t_done")
        h_ready = sem("hidden_ps_ready")
        gelu_done = sem("gelu_done")
        y_filled = sem("y_ps_filled")
        route_step = sem("route_step")
        route_exp = sem("route_exp")
        combt_done = sem("comb_t_done")
        acc_done = sem("acc_done")

        def at(chunk, per, k):
            v = chunk * per + k
            return max(v, 0) if isinstance(v, int) else v

        acc_order = ["e0", "e1", "b2"] + [f"e{e}" for e in range(2, NEXP)]

        LN_STEPS = [NT + 8, NT + 8, NT + 7]
        A_READ = {"k": (k_done, 4, 4), "v0": (v_done, 4, 2), "v1": (v_done, 4, 4), "out": (ln_step[0], LN_STEPS[0], 1),
                  "x1t": (x1t_done, 1, 1), "q0": (q_done, 8, 4), "q1": (q_done, 8, 8),
                  "att": (att_t_done, 1, 1), "o": (ln_step[1], LN_STEPS[1], 1)}
        for t in range(NT):
            A_READ[f"pv{t}"] = (att_done, 4, t + 1)
            for u in range(2):
                A_READ[f"sc{t}{u}"] = (shift_done, 8, 2 * t + u + 1)
                A_READ[f"pt{t}{u}"] = (pt_done, 8, 2 * t + u + 1)
        Y_READ = {"x2t": (x2t_done, 1, 1), "router": (route_step, 19, 1), "comb": (combt_done, 1, 1)}
        for name in acc_order:
            Y_READ[name] = (acc_done, 9, acc_order.index(name) + 1)

        def a_before(name):
            i = A_ORDER.index(name)
            return A_ORDER[i - 2 if i >= 2 else max(j for j in range(NA) if j % 2 == i)]

        def a_reader(name):
            return A_READ[a_before(name)][0]

        def a_read(c, name):
            _, per, k = A_READ[a_before(name)]
            return at(c, per, k if A_ORDER.index(name) >= 2 else k - per)

        def a_count(c, name):
            return at(c, NA, A_ORDER.index(name) + 1)

        def a_bank(name):
            return a_ps[A_ORDER.index(name) % 2]

        def y_reader(name):
            return Y_READ[Y_ORDER[Y_ORDER.index(name) - 1]][0]

        def y_read(c, name):
            i = Y_ORDER.index(name)
            _, per, k = Y_READ[Y_ORDER[i - 1]]
            return at(c, per, k if i else k - per)

        def y_count(c, name):
            return at(c, NY, Y_ORDER.index(name) + 1)

        def run(eng, iteration):
            first, last = max(START.values()), CHUNKS
            for it in range(first):
                iteration(it, it % 2)
            with eng.Fori(first, last, 2) as it:
                iteration(it, 0)
                iteration(it + 1, 1)
            for it in range(last, CHUNKS + max(START.values())):
                iteration(it, it % 2)

        def chunks_of(it):
            return {s: it - b for s, b in START.items()
                    if not isinstance(it, int) or 0 <= it - b < CHUNKS}

        block = ctx.enter_context(nc.Block())

        @block.sync
        def _(sp):
            sp.dma_start(par[:], params).then_inc(par_in, 16)
            sp.dma_start(xt[:, 0, :], x_t[0]).then_inc(xt_in, 16)
            sp.dma_start(ctxs[:], ctx_t[0]).then_inc(ctx_in, 16)
            sp.dma_start(xtok[:], x_tok[0]).then_inc(xtok_in, 16)
            sp.dma_start(w1s[:], w1).then_inc(w1_in, 16)
            sp.dma_start(w2s[:], w2).then_inc(w2_in, 16)

            def iteration(it, p):
                c = chunks_of(it)
                if "F" in c and not (isinstance(it, int) and it + 1 >= CHUNKS):
                    if "S" in c:
                        sp.wait_ge(c_ready, at(c["S"], C_USES, z_use(1) + 1))
                    sp.dma_start(xt[:, 1 - p, :], x_t[it + 1]).then_inc(xt_in, 16)
                if "O" in c:
                    sp.wait_ge(ln_out[2], at(c["O"], 4, 4))
                    sp.dma_start(out[c["O"]], obuf[:]).then_inc(stored, 16)
                if "A" in c and not (isinstance(it, int) and c["A"] + 1 >= CHUNKS):
                    sp.wait_ge(a_filled, a_count(c["A"], "v1"))
                    sp.dma_start(ctxs[:], ctx_t[c["A"] + 1]).then_inc(ctx_in, 16)
                    sp.wait_ge(ln_step[0], at(c["A"], LN_STEPS[0], 1))
                    sp.dma_start(xtok[:], x_tok[c["A"] + 1]).then_inc(xtok_in, 16)

            first, last = max(START.values()), CHUNKS
            for it in range(first):
                iteration(it, it % 2)
            with sp.Fori(first, last - 2, 2) as it:
                iteration(it, 0)
                iteration(it + 1, 1)
            for it in range(last - 2, CHUNKS + max(START.values())):
                iteration(it, it % 2)
            sp.wait_ge(stored, 16 * CHUNKS)

        @block.tensor
        def _(pe):
            pe.wait_ge(par_in, 16)
            pe.wait_ge(setup["dve"], 3)
            pe.matmul(f_ps[:, 0:D], pc("bv").to_broadcast([P, P]), pc("wo"), start=True, stop=False)
            pe.matmul(f_ps[:, 0:D], ones_row, pc("bo_row", rows=1), start=False, stop=True)\
                .then_inc(setup["pe"], 1)
            pe.wait_ge(setup["act"], 2)

            def hidden(c, units):
                for u in units:
                    pe.wait_ge(gelu_done, at(c, HID_UNITS, u - 1))
                    pe.matmul(h_ps[u % 2][:], w1s[:, u * P:(u + 1) * P], x2t[:], start=True, stop=True)\
                        .then_inc(h_ready, 1)

            def project(c, e):
                name = f"e{e}"
                pe.wait_ge(y_reader(name), y_read(c, name))
                pe.wait_ge(gelu_done, at(c, HID_UNITS, HB4 * (e + 1)))
                for t in range(NT):
                    for j in range(HB4):
                        u = HB4 * e + j
                        mm = pe.matmul(y_ps[:, t * P:(t + 1) * P], hid[:, u % HID_RING, t * P:(t + 1) * P],
                                       w2s[:, u * D:(u + 1) * D], start=j == 0, stop=j == HB4 - 1)
                mm.then_inc(y_filled, 1)

            def scores(c, t):
                pe.wait_ge(q_done, at(c, 8, 4 * (t // 2) + 4))
                if t == 0:
                    pe.wait_ge(k_done, at(c, 4, 4))
                for u in range(2):
                    name = f"sc{t}{u}"
                    pe.wait_ge(a_reader(name), a_read(c, name))
                    for g in range(2):
                        for s in range(2):
                            q = qm[:, 2 * u + g, (t % 2) * P + s * SEQ:(t % 2) * P + (s + 1) * SEQ]
                            k = km[:, :, t * P + s * SEQ:t * P + (s + 1) * SEQ]
                            mm = pe.matmul(a_bank(name)[s * SEQ:(s + 1) * SEQ, g * 256:(g + 1) * 256],
                                           q, k, start=True, stop=True)
                    mm.then_inc(a_filled, 1)

            def probs_transposed(c, t):
                pe.wait_ge(exp_done, at(c, NT, t + 1))
                for u in range(2):
                    name = f"pt{t}{u}"
                    pe.wait_ge(a_reader(name), a_read(c, name))
                    for k in range(4):
                        hp = 4 * u + k
                        mm = pe.transpose(a_bank(name)[:, k * P:(k + 1) * P],
                                          probs[:, t % 2, hp * P:(hp + 1) * P], ident)
                    mm.then_inc(a_filled, 1)

            def values(c, t):
                name = f"pv{t}"
                pe.wait_ge(a_reader(name), a_read(c, name))
                pe.wait_ge(pt_done, at(c, 8, 2 * t + 2))
                if t == 0:
                    pe.wait_ge(v_done, at(c, 4, 4))
                for hp in range(8):
                    for s in range(2):
                        mm = pe.matmul(a_bank(name)[s * SEQ:(s + 1) * SEQ, hp * 18:(hp + 1) * 18],
                                       probs_t[:, hp, s * SEQ:(s + 1) * SEQ], vv[:, (2 * t + s) * 8 + hp, :],
                                       start=True, stop=True)
                mm.then_inc(a_filled, 1)

            def q_proj(c, half):
                name = f"q{half}"
                pe.wait_ge(a_reader(name), a_read(c, name))
                if half == 0:
                    pe.wait_ge(x1t_done, at(c, 1, 1))
                pe.matmul(a_bank(name)[:, 0:256], pc("wq"), x1t[:, half * 256:(half + 1) * 256],
                          start=True, stop=True).then_inc(a_filled, 1)

            def iteration(it, p):
                c = chunks_of(it)
                for s in range(SLOTS):
                    if "S" in c:
                        S = c["S"]
                        if s == 0:
                            pe.wait_ge(split_done, at(S, 5, 5))
                        pe.wait_ge(input_done, at(S, UNITS, 2 * s))
                        pe.matmul(b_ps[:], select_bf[:, s:s + 1].to_broadcast([96, P]), bc3[:, 1 - p, :],
                                  start=True, stop=True).then_inc(b_ready, 1)
                        pe.wait_ge(c_taken, at(S, C_USES, c_use(s)))
                        pe.matmul(c_ps[:], select_bf[:, NSTATE + s:NSTATE + s + 1].to_broadcast([96, P]),
                                  bc3[:, 1 - p, :], start=True, stop=True).then_inc(c_ready, 1)
                        if s == 3:
                            for h in range(HALVES):
                                pe.wait_ge(c_taken, at(S, C_USES, z_use(h)))
                                pe.matmul(c_ps[:], pc("w_in", E_IN + h * P, E_IN + (h + 1) * P),
                                          xt[:, 1 - p, :], start=True, stop=True).then_inc(c_ready, 1)
                    if "M" in c:
                        M = c["M"]
                        if s == 0:
                            pe.wait_ge(y_reader("x2t"), y_read(M, "x2t"))
                            for t in range(NT):
                                pe.wait_ge(ln_out[1], at(M, 4, t + 1))
                                mm = pe.transpose(y_ps[:, t * P:(t + 1) * P], x2[:, t, :], ident)
                            mm.then_inc(y_filled, 1)
                    if "F" in c:
                        F = c["F"]
                        if s == 0:
                            pe.wait_ge(xt_in, at(F, 16, 16))
                            for h in range(HALVES):
                                if h == 0:
                                    pe.wait_ge(sp_parts, at(F, 4, 0))
                                else:
                                    pe.wait_ge(x_in_done, at(F, 2, 1))
                                pe.matmul(f_ps[:], pc("w_in", h * P, (h + 1) * P), xt[:, p, :],
                                          start=True, stop=True).then_inc(xproj_done, 1)
                        if s == 4:
                            for h in range(HALVES):
                                pe.wait_ge(silu_done, at(F, 2, h + 1))
                                mm = pe.matmul(f_ps[0:104, :], pc("w_xp", h * 104, (h + 1) * 104),
                                               xc[:, p, h, :], start=h == 0, stop=h == 1)
                            mm.then_inc(xproj_done, 1)
                        if s in (5, 6):
                            h = s - 5
                            if h == 0:
                                pe.wait_ge(split_done, at(F, 5, 2))
                                pe.wait_ge(dtlow_done, at(F, 1, 1))
                            else:
                                pe.wait_ge(sp_parts, at(F, 4, 2))
                            pe.matmul(f_ps[:], pc("w_dt_rows", h * P, (h + 1) * P, DTR, 96),
                                      dt_low, start=True, stop=True).then_inc(xproj_done, 1)
                    if "A" in c:
                        A = c["A"]
                        if s == 0:
                            pe.wait_ge(ctx_in, at(A, 16, 16))
                            pe.wait_ge(a_reader("k"), a_read(A, "k"))
                            pe.matmul(a_bank("k")[:], pc("wk"), ctxs[:], start=True, stop=True)\
                                .then_inc(a_filled, 1)
                            for v in range(2):
                                name = f"v{v}"
                                pe.wait_ge(a_reader(name), a_read(A, name))
                                for k in range(4):
                                    b = 4 * v + k
                                    for r in range(2):
                                        mm = pe.matmul(a_bank(name)[r * SEQ:(r + 1) * SEQ, k * P:(k + 1) * P],
                                                       ctxs[:, b * SEQ:(b + 1) * SEQ], pc("wv"),
                                                       start=True, stop=True)
                                mm.then_inc(a_filled, 1)
                        if s == 1:
                            pe.wait_ge(a_reader("out"), a_read(A, "out"))
                            pe.wait_ge(gate_step, at(A, 4, 4))
                            for t in range(NT):
                                for h in range(HALVES):
                                    mm = pe.matmul(a_bank("out")[:, t * P:(t + 1) * P],
                                                   gz[:, h, t * P:(t + 1) * P],
                                                   pc("w_out", h * D, (h + 1) * D), start=h == 0, stop=h == 1)
                            mm.then_inc(a_filled, 1)
                        if s == 3:
                            pe.wait_ge(a_reader("x1t"), a_read(A, "x1t"))
                            for t in range(NT):
                                pe.wait_ge(ln_out[0], at(A, 4, t + 1))
                                mm = pe.transpose(a_bank("x1t")[:, t * P:(t + 1) * P], x1[:, t, :], ident)
                            mm.then_inc(a_filled, 1)
                        if s == 4:
                            q_proj(A, 0)
                        if s == 5:
                            scores(A, 0)
                        if s == 6:
                            scores(A, 1)
                        if s == 7:
                            q_proj(A, 1)
                            probs_transposed(A, 0)
                        if s == 8:
                            values(A, 0)
                            probs_transposed(A, 1)
                            scores(A, 2)
                        if s == 9:
                            values(A, 1)
                            scores(A, 3)
                        if s == 11:
                            probs_transposed(A, 2)
                        if s == 12:
                            values(A, 2)
                            probs_transposed(A, 3)
                        if s == 13:
                            values(A, 3)
                        if s == 14:
                            pe.wait_ge(a_reader("att"), a_read(A, "att"))
                            pe.wait_ge(att_done, at(A, 4, 4))
                            for t in range(NT):
                                mm = pe.transpose(a_bank("att")[:, t * P:(t + 1) * P], att[:, t, :], ident)
                            mm.then_inc(a_filled, 1)
                    if "M" in c:
                        if s == 0:
                            pe.wait_ge(x2t_done, at(M, 1, 1))
                            pe.wait_ge(y_reader("router"), y_read(M, "router"))
                            for t in range(NT):
                                mm = pe.matmul(y_ps[:, t * NEXP:(t + 1) * NEXP], x2t[:, t * P:(t + 1) * P],
                                               pc("router"), start=True, stop=True)
                            mm.then_inc(y_filled, 1)
                        q, r = s // 4, s % 4
                        if r < 2:
                            hidden(M, range(8 * q + 4 * r, 8 * q + 4 * r + 4))
                        else:
                            project(M, 2 * q + r - 2)
                        if s == 4:
                            pe.wait_ge(y_reader("comb"), y_read(M, "comb"))
                            pe.wait_ge(route_step, at(M, 19, 19))
                            for t in range(NT):
                                mm = pe.transpose(y_ps[0:NEXP, t * P:(t + 1) * P], comb[:, t, :], ident)
                            mm.then_inc(y_filled, 1)
                        if s == 5:
                            pe.wait_ge(y_reader("b2"), y_read(M, "b2"))
                            pe.wait_ge(combt_done, at(M, 1, 1))
                            for t in range(NT):
                                mm = pe.matmul(y_ps[:, t * P:(t + 1) * P], comb_t[:, t * P:(t + 1) * P],
                                               pc("b2_rows", rows=NEXP), start=True, stop=True)
                            mm.then_inc(y_filled, 1)
                    if "A" in c and s == 14:
                        pe.wait_ge(a_reader("o"), a_read(A, "o"))
                        pe.wait_ge(att_t_done, at(A, 1, 1))
                        for t in range(NT):
                            mm = pe.matmul(a_bank("o")[:, t * P:(t + 1) * P], x1t[:, t * P:(t + 1) * P],
                                           pc("wo"), start=True, stop=True)
                        mm.then_inc(a_filled, 1)

            pe.wait_ge(setup["dve"], 10)
            pe.wait_ge(w1_in, 16)
            pe.wait_ge(w2_in, 16)
            run(pe, iteration)

        @block.scalar
        def _(act):
            act.wait_ge(par_in, 16)
            act.activation(neg_a[:], pc("a_log"), ACT.Exp).then_inc(setup["act"], 1)
            act.wait_ge(setup["pe"], 1)
            act.activation(bo[:], f_ps[:, 0:D], ACT.Copy).then_inc(setup["act"], 1)
            act.wait_ge(setup["dve"], 10)

            def per_seq(ap):
                return ap.rearrange("p (b t) -> p b t", b=NB)

            def decays(S, p, n):
                for h in range(HALVES):
                    u = 2 * n + h
                    act.wait_ge(scan_done, at(S, UNITS, u - DECAY_RING + 1))
                    if u == 0:
                        act.wait_ge(dt_done, at(S, 2, 2))
                    act.activation(per_seq(decay[:, u % DECAY_RING, :])[:, :, 1:],
                                   per_seq(dt[:, p, h, :])[:, :, 1:], ACT.Exp,
                                   scale=neg_a[:, h * NSTATE + n:h * NSTATE + n + 1]).then_inc(decay_done, 1)

            def gelus(M, units):
                for u in units:
                    act.wait_ge(h_ready, at(M, HID_UNITS, u + 1))
                    if u % HB4 == 0:
                        e = u // HB4 - 2
                        k = Y_ORDER.index(f"e{e}") + 1 if e >= 0 else Y_ORDER.index(f"e{e + NEXP}") + 1 - NY
                        act.wait_ge(y_filled, at(M, NY, k))
                    act.activation(hid[:, u % HID_RING, :], h_ps[u % 2][:], ACT.Gelu_apprx_tanh,
                                   bias=pc("b1", u, u + 1)).then_inc(gelu_done, 1)

            def q_parts(A, half):
                act.wait_ge(a_filled, a_count(A, f"q{half}"))
                for g in range(4):
                    act.activation(qm[:, g, :], a_bank(f"q{half}")[:, 0:256], ACT.Identity,
                                   scale=qscale[:, 2 * g:2 * g + 1], bias=qscale[:, 2 * g + 1:2 * g + 2])\
                        .then_inc(q_done, 1)


            def exp_probs(A, t):
                act.wait_ge(shift_done, at(A, 8, 2 * t + 2))
                act.activation(probs[:, t % 2, :], probs[:, t % 2, :], ACT.Exp).then_inc(exp_done, 1)

            def pt_copies(A, t):
                for u in range(2):
                    name = f"pt{t}{u}"
                    act.wait_ge(a_filled, a_count(A, name))
                    act.activation(probs_t[:, 4 * u:4 * u + 4, :], a_bank(name)[:].rearrange("p (k q) -> p k q", k=4),
                                   ACT.Copy).then_inc(pt_done, 1)

            def iteration(it, p):
                c = chunks_of(it)
                for s in range(SLOTS):
                    if "M" in c and s == 2:
                        act.wait_ge(route_step, at(c["M"], 19, 13))
                        act.activation(rm[:, 3, :], rm[:, 2, :], ACT.Exp).then_inc(route_exp, 1)
                    if "S" in c:
                        S = c["S"]
                        for n in DECAY_SLOTS.get(s, []):
                            decays(S, 1 - p, n)
                        act.wait_ge(c_ready, at(S, C_USES, c_use(s) + 1))
                        act.wait_ge(prod_done, at(S, UNITS, 2 * s - 2))
                        act.activation(c_all[:, s % 2, :], c_ps[:], ACT.Copy).then_inc(c_taken, 1)
                    if "M" in c and s == 0:
                        M = c["M"]
                        act.wait_ge(y_filled, y_count(M, "x2t"))
                        act.wait_ge(h_ready, at(M, HID_UNITS, 0))
                        act.activation(x2t[:], y_ps[:], ACT.Copy).then_inc(x2t_done, 1)
                    if "F" in c:
                        F = c["F"]
                        if s == 0:
                            for h in range(HALVES):
                                act.wait_ge(xproj_done, at(F, NF, h + 1))
                                if h == 0:
                                    act.wait_ge(input_done, at(F - 1, UNITS, 0))
                                act.activation(du[:, p, h, :], f_ps[:], ACT.Copy).then_inc(x_in_done, 1)
                        if s == 4:
                            act.wait_ge(xproj_done, at(F, NF, 3))
                            act.activation(dt_low, f_ps[96:96 + DTR, :], ACT.Copy)\
                                .then_inc(dtlow_done, 1)
                        if s in (5, 6):
                            h = s - 5
                            act.wait_ge(xproj_done, at(F, NF, 4 + h))
                            if h == 0:
                                act.wait_ge(split_done, at(F, 5, 5))
                            act.activation(dt[:, p, h, :], f_ps[:], ACT.Relu, bias=pc("b_dt", h, h + 1))\
                                .then_inc(sp_parts, 1)
                            act.activation(du[:, p, h, :], f_ps[:], ACT.Abs, bias=pc("b_dt", h, h + 1))\
                                .then_inc(sp_parts, 1)
                    if "A" in c:
                        A = c["A"]
                        if s == 0:
                            act.wait_ge(a_filled, a_count(A, "k"))
                            for j in range(4):
                                act.activation(km[:, j, :], a_bank("k")[:], ACT.Identity,
                                               scale=pc("head_mask", j, j + 1), bias=kbias[:, j:j + 1])\
                                    .then_inc(k_done, 1)
                            for v in range(2):
                                act.wait_ge(a_filled, a_count(A, f"v{v}"))
                                src = a_bank(f"v{v}")[:].rearrange("p (b k r d) -> p (b k) r d", b=4, k=8, r=2)
                                dst = vv[:, 32 * v:32 * v + 32, :].rearrange("p k (r d) -> p k r d", r=2)
                                for r in range(2):
                                    act.activation(dst[:, :, r, 0:DH], src[:, :, r, :], ACT.Copy,
                                                   scale=pc("half_mask", r, r + 1)).then_inc(v_done, 1)
                        if s == 4:
                            q_parts(A, 0)
                        if s == 6:
                            exp_probs(A, 0)
                        if s == 7:
                            exp_probs(A, 1)
                            q_parts(A, 1)
                            pt_copies(A, 0)
                        if s == 8:
                            pt_copies(A, 1)
                        if s == 10:
                            exp_probs(A, 2)
                        if s == 11:
                            exp_probs(A, 3)
                            pt_copies(A, 2)
                        if s == 12:
                            pt_copies(A, 3)
                        if s == 14:
                            act.wait_ge(a_filled, a_count(A, "att"))
                            act.activation(x1t[:], a_bank("att")[:], ACT.Copy).then_inc(att_t_done, 1)
                    if "F" in c and s == 7:
                        for h in range(HALVES):
                            act.wait_ge(sp_parts, at(F, 4, 2 * h + 2))
                            act.activation(du[:, p, h, :], du[:, p, h, :], ACT.Exp, scale=-1.0).then_inc(sp_exp, 1)
                        for h in range(HALVES):
                            act.wait_ge(sp_exp, at(F, 2, h + 1))
                            act.activation(du[:, p, h, :], du[:, p, h, :], ACT.Ln, bias=1.0).then_inc(sp_ln, 1)
                    if s == 3:
                        if "F" in c:
                            for h in range(HALVES):
                                act.wait_ge(conv_done, at(F, 8, 7 + h))
                                act.activation(xc[:, p, h, :], xc[:, p, h, :], ACT.Silu).then_inc(silu_done, 1)
                        if "S" in c:
                            for h in range(HALVES):
                                act.wait_ge(c_ready, at(S, C_USES, z_use(h) + 1))
                                if h == 0:
                                    act.wait_ge(a_filled, a_count(S - 1, "out"))
                                act.activation(gz[:, h, :], c_ps[:], ACT.Silu).then_inc(c_taken, 1)
                        if "A" in c:
                            act.wait_ge(a_filled, a_count(c["A"], "x1t"))
                            act.activation(x1t[:], a_bank("x1t")[:], ACT.Copy).then_inc(x1t_done, 1)
                    if "M" in c and s % 4 < 2:
                        gelus(c["M"], range(8 * (s // 4) + 4 * (s % 4), 8 * (s // 4) + 4 * (s % 4) + 4))

            run(act, iteration)

        @block.vector
        def _(dve):
            dve.memset(decay[:], 0.0).then_inc(setup["dve"], 1)
            dve.memset(ones_row, 1.0).then_inc(setup["dve"], 1)
            dve.memset(vv[:], 0.0).then_inc(setup["dve"], 1)
            dve.wait_ge(par_in, 16)
            dve.tensor_copy(select_bf[:], pc("select", rows=96)).then_inc(setup["dve"], 1)
            dve.tensor_scalar(kbias[:], pc("head_mask"), pc("bk"), None, ALU.mult).then_inc(setup["dve"], 1)
            dve.wait_ge(setup["dve"], 3)
            for r in range(2):
                one = vv[:, :, r * (DH + 1) + DH]
                dve.tensor_scalar(one, one, pc("half_mask", r, r + 1), None,
                                  ALU.add).then_inc(setup["dve"], 1)
            qv = qscale[:].rearrange("p (g k) -> p g k", k=2)
            dve.tensor_scalar(qv[:, :, 0], pc("group_mask"), float(DH) ** -0.5, None, ALU.mult)\
                .then_inc(setup["dve"], 1)
            dve.tensor_scalar(qv[:, :, 1], pc("group_mask"), pc("bq"), float(DH) ** -0.5, ALU.mult, ALU.mult)\
                .then_inc(setup["dve"], 1)
            dve.wait_ge(setup["act"], 1)
            dve.tensor_scalar(neg_a[:], neg_a[:], -1.0, None, ALU.mult).then_inc(setup["dve"], 1)

            def ln_stats(c, i, src, made, made_at):
                for t in range(NT):
                    if t == 0:
                        dve.wait_ge(made, made_at)
                    dve.bn_stats(ln_st[:, i, t, :], src[:, t, :]).then_inc(ln_step[i], 1)
                st, a, b = ln_st[:, i], ln_tmp[:, 0], ln_tmp[:, 1]
                mean, ve = ln_mean[:, i, :], ln_ve[:, i, :]

                def step(n, after, op, *args):
                    dve.wait_ge(ln_step[i], at(c, LN_STEPS[i], LN_STEPS[i] - 7 + after))
                    op(*args).then_inc(ln_step[i], 1)

                step(1, 0, dve.tensor_tensor, mean, st[:, :, 1], st[:, :, 4], ALU.add)
                step(2, 0, dve.tensor_tensor, a, st[:, :, 1], st[:, :, 4], ALU.subtract)
                step(3, 0, dve.tensor_tensor, b, st[:, :, 2], st[:, :, 5], ALU.add)
                step(4, 1, dve.tensor_scalar, mean, mean, 0.5, None, ALU.mult)
                step(5, 2, dve.scalar_tensor_tensor, a, a, 0.25, a, ALU.mult, ALU.mult)
                step(6, 5, dve.scalar_tensor_tensor, ve, b, 1.0 / D, a, ALU.mult, ALU.add)
                step(7, 6, dve.tensor_scalar, ve, ve, EPS, None, ALU.add)

            def ln_scale(c, i, dst, src):
                dve.wait_ge(ln_rstd[i], at(c, 1, 1))
                for t in range(NT):
                    dve.tensor_scalar(dst[:, t, :], src[:, t, :], ln_mean[:, i, t:t + 1], ln_rs[:, i, t:t + 1],
                                      ALU.subtract, ALU.mult).then_inc(ln_out[i], 1)

            def group_sum(S, k, h):
                idx = 2 * k + h
                dve.wait_ge(prod_done, at(S, UNITS, 2 * (GROUP * k + GROUP - 1) + h + 1))
                if k:
                    dve.wait_ge(sum_done, at(S, 6, idx - 1))
                lo = 0 if k else 1
                ins = dve.tensor_reduce(prod[:, (idx + 2) % PROD_RING, 0, :],
                                        prod[:, idx % PROD_RING, lo:, :].rearrange("p n t -> p t n"),
                                        AX.X, ALU.add)
                ins.then_inc(last_sum if k == NGROUP - 1 else sum_done, 1)

            def conv_taps(F, p, taps):
                for i, k in taps:
                    sh = NCONV - 1 - k
                    for h in range(HALVES):
                        w = pc("conv_w", h * NCONV + k, h * NCONV + k + 1)
                        if i == 0:
                            dve.wait_ge(x_in_done, at(F, 2, h + 1))
                            dve.tensor_scalar(xc[:, p, h, :], du[:, p, h, :], w, pc("conv_b", h, h + 1),
                                              ALU.mult, ALU.add).then_inc(conv_done, 1)
                        else:
                            dve.wait_ge(conv_done, at(F, 8, 2 * i + h - 1))
                            o = xc[:, p, h, :].rearrange("p (b t) -> p b t", b=NB)[:, :, sh:]
                            a = du[:, p, h, :].rearrange("p (b t) -> p b t", b=NB)[:, :, 0:SEQ - sh]
                            dve.scalar_tensor_tensor(o, a, w, o, ALU.mult, ALU.add).then_inc(conv_done, 1)

            def shift(A, t):
                for u in range(2):
                    name = f"sc{t}{u}"
                    v = a_bank(name)[:].rearrange("p (h k) -> p h k", h=8)
                    dve.wait_ge(a_filled, a_count(A, name))
                    dve.tensor_reduce(mx[:, u, :], v, AX.X, ALU.max).then_inc(max_done, 1)
                    dve.wait_ge(max_done, at(A, 8, 2 * t + u + 1))
                    dve.tensor_tensor(probs[:, t % 2, u * TOK:(u + 1) * TOK].rearrange("p (h k) -> p h k", h=8), v,
                                      mx[:, u, :].unsqueeze(2).to_broadcast([P, 8, SEQ]), ALU.subtract)\
                        .then_inc(shift_done, 1)


            def normalise(A, t):
                name = f"pv{t}"
                v = a_bank(name)[:, 0:HEADS * (DH + 1)].rearrange("p (h d) -> p h d", h=HEADS)
                dve.wait_ge(a_filled, a_count(A, name))
                dve.reciprocal(rden[:], v[:, :, DH]).then_inc(rden_done, 1)
                dve.wait_ge(rden_done, at(A, 4, t + 1))
                dve.tensor_tensor(att[:, t, :].rearrange("p (h d) -> p h d", h=HEADS), v[:, :, 0:DH],
                                  rden[:].unsqueeze(2).to_broadcast([P, HEADS, DH]), ALU.mult).then_inc(att_done, 1)

            def over_experts(i):
                return rm[:, i, :].unsqueeze(2).to_broadcast([P, NT, NEXP])

            def route(M, n, op, *args):
                if n > 1:
                    dve.wait_ge(route_step, at(M, 19, n - 1))
                op(*args).then_inc(route_step, 1)

            def choose_experts(M):
                tie = pc("tie_order").unsqueeze(1).to_broadcast([P, NT, NEXP])
                dve.wait_ge(y_filled, y_count(M, "router"))
                route(M, 1, dve.tensor_copy, rl[:, 0], y_ps[:, 0:NT * NEXP].rearrange("p (t e) -> p t e", t=NT))
                for i in range(2):
                    n = 2 + 6 * i
                    route(M, n, dve.tensor_reduce, rm[:, i, :], rl[:, 0], AX.X, ALU.max)
                    route(M, n + 1, dve.tensor_tensor, rl[:, 3], rl[:, 0], over_experts(i), ALU.is_equal)
                    route(M, n + 2, dve.tensor_tensor, rl[:, 3], rl[:, 3], tie, ALU.mult)
                    route(M, n + 3, dve.tensor_reduce, rm[:, 4, :], rl[:, 3], AX.X, ALU.max)
                    route(M, n + 4, dve.tensor_tensor, rl[:, 1 + i], rl[:, 3], over_experts(4), ALU.is_equal)
                    if i == 0:
                        route(M, 7, dve.scalar_tensor_tensor, rl[:, 0], rl[:, 1], -1e30, rl[:, 0],
                              ALU.mult, ALU.add)
                route(M, 13, dve.tensor_tensor, rm[:, 2, :], rm[:, 1, :], rm[:, 0, :], ALU.subtract)

            def weigh_experts(M):
                dve.wait_ge(route_exp, at(M, 1, 1))
                route(M, 14, dve.tensor_scalar, rm[:, 4, :], rm[:, 3, :], 1.0, None, ALU.add)
                route(M, 15, dve.reciprocal, rm[:, 4, :], rm[:, 4, :])
                route(M, 16, dve.tensor_tensor, rm[:, 5, :], rm[:, 3, :], rm[:, 4, :], ALU.mult)
                route(M, 17, dve.tensor_tensor, rl[:, 1], rl[:, 1], over_experts(4), ALU.mult)
                route(M, 18, dve.tensor_tensor, rl[:, 2], rl[:, 2], over_experts(5), ALU.mult)
                route(M, 19, dve.tensor_tensor, comb[:], rl[:, 1], rl[:, 2], ALU.add)

            def combine(M, e):
                dve.wait_ge(y_filled, y_count(M, f"e{e}"))
                if e == 0:
                    dve.wait_ge(route_step, at(M, 19, 19))
                    dve.wait_ge(ln_out[2], at(M - 1, 4, 4))
                for t in range(NT):
                    if t == 0 and e:
                        dve.wait_ge(acc_done, at(M, 9, acc_order.index(f"e{e}")))
                    ins = dve.scalar_tensor_tensor(acc[:, t, :], y_ps[:, t * P:(t + 1) * P], comb[:, t, e:e + 1],
                                                   (acc if e else x2)[:, t, :], ALU.mult, ALU.add)
                ins.then_inc(acc_done, 1)

            def iteration(it, p):
                c = chunks_of(it)
                for s in range(SLOTS):
                    if "S" in c:
                        S = c["S"]
                        for h in range(HALVES):
                            u = 2 * s + h
                            if h == 0:
                                if s == 0:
                                    dve.wait_ge(du_done, at(S, 2, 2))
                                dve.wait_ge(b_ready, at(S, NSTATE, s + 1))
                            dve.wait_ge(prod_done, at(S, UNITS, u - SCAN_RING + 1))
                            dve.tensor_tensor(state[:, u % SCAN_RING, :], b_ps[:], du[:, 1 - p, h, :], ALU.mult)\
                                .then_inc(input_done, 1)
                        for h in range(HALVES):
                            u = 2 * s + h
                            dve.wait_ge(decay_done, at(S, UNITS, u + 1))
                            dve.wait_ge(input_done, at(S, UNITS, u + 1))
                            dve.tensor_tensor_scan(state[:, u % SCAN_RING, :], decay[:, u % DECAY_RING, :],
                                                   state[:, u % SCAN_RING, :], 0.0, ALU.mult, ALU.add)\
                                .then_inc(scan_done, 1)
                        if s in (4, 8, 12):
                            for h in range(HALVES):
                                group_sum(S, s // GROUP - 1, h)
                    if "O" in c and s == 0:
                        dve.wait_ge(stored, at(c["O"], 16, 0))
                        ln_scale(c["O"], 2, obuf, acc)
                    if "A" in c:
                        A = c["A"]
                        if s == 0:
                            for h in range(HALVES):
                                group_sum(A, NGROUP - 1, h)
                            for h in range(HALVES):
                                y = prod[:, h, 0, :]
                                dve.wait_ge(last_sum, at(A, 2, h + 1))
                                dve.scalar_tensor_tensor(y, xc[:, p, h, :], pc("skip_d", h, h + 1), y,
                                                         ALU.mult, ALU.add).then_inc(gate_step, 1)
                            for h in range(HALVES):
                                y = prod[:, h, 0, :]
                                dve.wait_ge(gate_step, at(A, 4, h + 1))
                                dve.tensor_tensor(gz[:, h, :], y, gz[:, h, :], ALU.mult).then_inc(gate_step, 1)
                        if s == 1:
                            dve.wait_ge(a_filled, a_count(A, "out"))
                            dve.wait_ge(xtok_in, at(A, 16, 16))
                            dve.tensor_tensor(x1[:], a_bank("out")[:].rearrange("p (t d) -> p t d", t=NT), xtok[:],
                                              ALU.add).then_inc(ln_step[0], 1)
                            ln_stats(A, 0, x1, ln_step[0], at(A, LN_STEPS[0], 1))
                    if "F" in c:
                        F = c["F"]
                        if s == 1:
                            dve.wait_ge(gate_step, at(F - 2, 4, 4))
                            conv_taps(F, p, [(0, 3), (1, 2)])
                        if s == 2:
                            conv_taps(F, p, [(2, 1), (3, 0)])
                        if s == 4:
                            r1 = du[0:96, p, 0, :]
                            t2 = du[0:96, p, 1, 0:TOK // 2].bitcast(BF16)
                            dve.wait_ge(xproj_done, at(F, NF, 3))
                            dve.wait_ge(c_ready, at(F - 1, C_USES, 0))
                            dve.tensor_copy(bc3[:, p, :], f_ps[0:96, :]).then_inc(split_done, 1)
                            dve.wait_ge(split_done, at(F, 5, 1))
                            dve.tensor_tensor(r1, f_ps[0:96, :], bc3[:, p, :], ALU.subtract).then_inc(split_done, 1)
                            dve.wait_ge(split_done, at(F, 5, 2))
                            dve.tensor_copy(bc3[32:64, p, :], r1[32:64]).then_inc(split_done, 1)
                            dve.tensor_copy(t2[64:96], r1[64:96]).then_inc(split_done, 1)
                            dve.wait_ge(split_done, at(F, 5, 4))
                            dve.tensor_tensor(bc3[64:96, p, :], r1[64:96], t2[64:96], ALU.subtract)\
                                .then_inc(split_done, 1)
                        if s == 8:
                            for h in range(HALVES):
                                dve.wait_ge(sp_ln, at(F, 2, h + 1))
                                dve.tensor_tensor(dt[:, p, h, :], dt[:, p, h, :], du[:, p, h, :], ALU.add)\
                                    .then_inc(dt_done, 1)
                            for h in range(HALVES):
                                dve.wait_ge(dt_done, at(F, 2, h + 1))
                                dve.tensor_tensor(du[:, p, h, :], dt[:, p, h, :], xc[:, p, h, :], ALU.mult)\
                                    .then_inc(du_done, 1)
                    if "M" in c:
                        M = c["M"]
                        if s == 1:
                            choose_experts(M)
                    late(c, s)

            def late(c, s):
                if "A" in c:
                    A = c["A"]
                    if s == 2:
                        ln_scale(A, 0, x1, x1)
                    if s == 5:
                        shift(A, 0)
                    if s == 6:
                        shift(A, 1)
                    if s == 8:
                        if "O" in c:
                            dve.wait_ge(stored, at(c["O"], 16, 16))
                        normalise(A, 0)
                        shift(A, 2)
                    if s == 9:
                        normalise(A, 1)
                        shift(A, 3)
                    if s == 12:
                        normalise(A, 2)
                    if s == 13:
                        normalise(A, 3)
                    if s == 15:
                        dve.wait_ge(a_filled, a_count(A, "o"))
                        dve.wait_ge(x1_biased, at(A, 1, 1))
                        dve.tensor_tensor(x2[:], a_bank("o")[:].rearrange("p (t d) -> p t d", t=NT), x1[:],
                                          ALU.add).then_inc(ln_step[1], 1)
                        ln_stats(A, 1, x2, ln_step[1], at(A, LN_STEPS[1], 1))
                if "M" in c:
                    M = c["M"]
                    if s == 4:
                        dve.wait_ge(y_filled, y_count(M, "comb"))
                        dve.tensor_copy(comb_t, y_ps[0:NEXP, :]).then_inc(combt_done, 1)
                    if s == 5:
                        dve.wait_ge(y_filled, y_count(M, "b2"))
                        dve.wait_ge(acc_done, at(M, 9, 2))
                        dve.tensor_tensor(acc[:], y_ps[:].rearrange("p (t d) -> p t d", t=NT), acc[:], ALU.add)\
                            .then_inc(acc_done, 1)
                    if s == 2:
                        weigh_experts(M)
                    if s % 4 >= 2:
                        combine(M, 2 * (s // 4) + s % 4 - 2)
                if s == SLOTS - 1:
                    if "M" in c:
                        ln_stats(c["M"], 2, acc, acc_done, at(c["M"], 9, 9))
                    if "A" in c:
                        ln_scale(c["A"], 1, x2, x2)

            run(dve, iteration)

        @block.gpsimd
        def _(pool):
            pool.memset(half_pow[:], -0.5).then_inc(setup["pool"], 1)
            pool.wait_ge(setup["pool"], 1)
            pool.wait_ge(setup["act"], 2)

            def rstd(c, i):
                pool.wait_ge(ln_step[i], at(c, LN_STEPS[i], LN_STEPS[i]))
                pool.tensor_tensor(ln_rs[:, i, :], ln_ve[:, i, :], half_pow[:], ALU.pow).then_inc(ln_rstd[i], 1)

            def iteration(it, p):
                c = chunks_of(it)
                for s in range(SLOTS):
                    if "S" in c:
                        S = c["S"]
                        k = s // GROUP
                        for h in range(HALVES):
                            u = 2 * s + h
                            idx = 2 * k + h
                            if s % GROUP == 0:
                                if k == 0:
                                    pool.wait_ge(sum_done, at(S - 1, 6, 5 + h))
                                elif k == 1:
                                    pool.wait_ge(last_sum, at(S - 1, 2, 1 + h))
                                else:
                                    pool.wait_ge(sum_done, at(S, 6, idx - 4 + 1))
                            if h == 0:
                                pool.wait_ge(c_taken, at(S, C_USES, c_use(s) + 1))
                            pool.wait_ge(scan_done, at(S, UNITS, u + 1))
                            pool.tensor_tensor(prod[:, idx % PROD_RING, 1 + s % GROUP, :],
                                               state[:, u % SCAN_RING, :], c_all[:, s % 2, :], ALU.mult)\
                                .then_inc(prod_done, 1)
                    if "A" in c:
                        A = c["A"]
                        if s == 1:
                            rstd(A, 0)
                        if s == 4:
                            pool.wait_ge(a_filled, a_count(A, "x1t"))
                            pool.tensor_tensor(x1[:], x1[:], bo[:].unsqueeze(1).to_broadcast([P, NT, D]),
                                               ALU.add).then_inc(x1_biased, 1)
                        if s == 15:
                            rstd(A, 1)
                    if "M" in c and s == 15:
                        rstd(c["M"], 2)

            run(pool, iteration)


def kernel(**inputs):
    import numpy as np
    import concourse.bacc as bacc
    from concourse.bass_utils import run_bass_kernel_spmd

    a = {k: np.asarray(v) for k, v in inputs.items()}

    def halves(m):
        return m.reshape(HALVES, P, -1).transpose(1, 0, 2).reshape(P, -1)

    params = np.zeros((P, NCOLS), np.float32)

    def put(name, m, row0=0):
        lo = COLS[name][0]
        params[row0:row0 + m.shape[0], lo:lo + m.shape[1]] = m

    rows = np.arange(P)[:, None]
    put("conv_w", halves(a["L0_attn_conv_w"]))
    put("conv_b", halves(a["L0_attn_conv_b"][:, None]))
    put("b_dt", halves(a["L0_attn_b_dt"][:, None]))
    put("skip_d", halves(a["L0_attn_D"][:, None]))
    put("a_log", halves(a["L0_attn_A_log"]))
    put("bq", a["L0_xattn_wq_b"][:, None])
    put("bk", a["L0_xattn_wk_b"][:, None])
    put("bv", a["L0_xattn_wv_b"][:, None])
    put("b1", a["L0_ffn_fc1_b"].reshape(NEXP * HB4, P).T)
    put("router", a["L0_ffn_router_w"].T)
    put("group_mask", (rows // 32 == np.arange(4)).astype(np.float32))
    put("head_mask", (rows // DH % 4 == np.arange(4)).astype(np.float32))
    put("half_mask", (rows // 64 == np.arange(2)).astype(np.float32))
    put("ident", np.eye(P, dtype=np.float32))
    put("bo_row", a["L0_xattn_wo_b"][None])
    put("b2_rows", a["L0_ffn_fc2_b"])
    put("w_dt_rows", a["L0_attn_W_dt"].T, 96)
    put("select", (np.arange(96)[:, None] % 32 == np.arange(32)).astype(np.float32))
    put("tie_order", np.tile(np.arange(NEXP, 0, -1, dtype=np.float32), (P, 1)))
    xp = a["L0_attn_W_xp"].T
    bc, low = xp[:, DTR:], xp[:, :DTR]
    put("w_xp", halves(np.concatenate([bc, bc, bc, low], 1)))
    put("w_in", a["L0_attn_W_in"].T)
    put("w_out", halves(a["L0_attn_W_out"].T))
    for n in "qkvo":
        put(f"w{n}", a[f"L0_xattn_w{n}_w"].T)

    def transposed(x):
        return np.ascontiguousarray(x.reshape(CHUNKS, TOK, D).transpose(0, 2, 1))

    arrays = {
        "x_t": transposed(a["x"]),
        "x_tok": np.ascontiguousarray(a["x"].reshape(CHUNKS, NT, P, D).transpose(0, 2, 1, 3)),
        "ctx_t": transposed(a["ctx_1024"]),
        "params": params,
        "w1": np.ascontiguousarray(a["L0_ffn_fc1_w"].transpose(2, 0, 1).reshape(D, NEXP * HID)),
        "w2": np.ascontiguousarray(
            a["L0_ffn_fc2_w"].reshape(NEXP, D, HB4, P).transpose(3, 0, 2, 1).reshape(P, NEXP * HB4 * D)),
    }
    nc = bacc.Bacc("TRN2", target_bir_lowering=False, num_devices=1)
    args = [nc.dram_tensor(n, v.shape, mybir.dt.from_np(v.dtype), kind="ExternalInput").ap()
            for n, v in arrays.items()]
    out = nc.dram_tensor("out", (CHUNKS, P, NT, D), mybir.dt.float32, kind="ExternalOutput").ap()
    decoder_layer(nc, *args, out)
    r = run_bass_kernel_spmd(nc, [arrays], core_ids=[0])
    y = r.results[0]["out"]
    return np.ascontiguousarray(y.transpose(0, 2, 1, 3)).reshape(BATCH, SEQ, D)
```

```python
from contextlib import ExitStack

import concourse.bass as bass
from concourse import mybir

BATCH, SEQ, D = 128, 64, 128
E_IN, NSTATE, NCONV, DTR = 256, 16, 4, 8
HEADS, DH = 16, 8
NEXP, HID = 8, 512
P = 128
TOK = 512
CHUNKS = BATCH * SEQ // TOK
NB = TOK // SEQ
NT = TOK // P
HALVES = E_IN // P
HB4 = HID // P
SLOTS = NSTATE
EPS = 1e-5

START = {"F": 0, "S": 1, "A": 2, "M": 3, "O": 4}

COLS = {}
_n = 0
for _name, _w in [("conv_w", HALVES * NCONV), ("conv_b", HALVES), ("b_dt", HALVES), ("skip_d", HALVES),
                  ("a_log", HALVES * NSTATE), ("bq", 1), ("bk", 1), ("bv", 1), ("b1", NEXP * HB4),
                  ("router", NEXP), ("group_mask", 4), ("head_mask", 4), ("half_mask", 2),
                  ("ident", P), ("w_dt_rows", E_IN), ("select", 32),
                  ("tie_order", NEXP), ("w_xp", HALVES * 104), ("w_in", 2 * E_IN), ("w_out", HALVES * D),
                  ("wq", D), ("wk", D), ("wv", D), ("wo", D)]:
    COLS[_name] = (_n, _n + _w)
    _n += _w
NCOLS = _n
COLS["b2_rows"] = (COLS["w_dt_rows"][0], COLS["w_dt_rows"][0] + D)
COLS["bo_row"] = (COLS["w_dt_rows"][0] + D, COLS["w_dt_rows"][0] + 2 * D)

DECAY_SLOTS = {2: [3, 4], 3: [5, 6], 6: [7, 8], 7: [9, 10], 10: [11, 12], 11: [13, 14], 14: [15]}
FIRST_DECAYS = {14: [0], 15: [1, 2]}
HIDDEN_SLOTS = {0: 0, 1: 4, 4: 8, 5: 12, 8: 16, 9: 20, 12: 24, 13: 28}
EARLY_B = (1, 8, 9, 10, 11, 12, 13, 14)
EARLY_C = (10, 11, 14)
PROJECT_SLOTS = {2: 0, 3: 1, 6: 2, 7: 3, 10: 4, 11: 5, 14: 6, 15: 7}
UNITS = NSTATE * HALVES
ADDS = UNITS - HALVES
DECAY_RING, SCAN_RING, C_RING = 8, 4, 4
HID_UNITS = NEXP * HB4
HID_RING = 8

A_ORDER = ["k", "out", "v0", "x1t", "q0", "v1", "sc00", "sc01", "sc10", "sc11", "q1", "pt00", "pt01",
           "sc20", "sc21", "pt10", "pt11", "sc30", "sc31", "pt20", "pt21", "pt30", "pt31", "att", "o"]
NA = len(A_ORDER)
Y_ORDER = ["x2t", "router", "e0", "e1", "comb", "b2", "e2", "e3", "e4", "e5", "e6", "e7"]
NY = len(Y_ORDER)
NF = 5


def decoder_layer(nc, x_t, x_tok, ctx_t, params, w1, w2, out):
    F32, F32R, BF16 = mybir.dt.float32, mybir.dt.float32r, mybir.dt.bfloat16
    ALU, ACT, AX = mybir.AluOpType, mybir.ActivationFunctionType, mybir.AxisListType

    ctx = ExitStack()
    with ctx:
        def sb(name, shape, dt=F32):
            return ctx.enter_context(nc.sbuf_tensor(name, shape, dt))

        def pb(name):
            return ctx.enter_context(nc.psum_tensor(name, [P, TOK], F32))

        def sem(name):
            return ctx.enter_context(nc.semaphore(name))

        par = sb("par", [P, NCOLS])
        w1_hi = sb("w1_hi", [P, HID_UNITS * P], F32R)
        w1_lo = sb("w1_lo", [P, HID_UNITS * P], F32R)
        w2s = sb("w2s", [P, HID_UNITS * D])
        select_bf = sb("select_bf", [96, 32], BF16)
        neg_a = sb("neg_a", [P, HALVES * NSTATE])
        qscale = sb("qscale", [P, 8])
        kbias = sb("kbias", [P, 4])
        bo = sb("bo", [P, D])
        half_pow = sb("half_pow", [P, NT])
        ones, warm = sb("ones", [P, 1]), sb("warm", [P, 1])
        xt = sb("xt", [P, 2, TOK])
        dt = sb("dt", [P, 2, HALVES, TOK])
        du = sb("du", [P, 2, HALVES, TOK])
        xc = sb("xc", [P, 2, HALVES, TOK])
        bc3 = sb("bc3", [96, 2, TOK], BF16)
        low = sb("low", [P, TOK])
        dt_low, comb_t = low[96:96 + DTR, :], low[0:NEXP, :]
        gz = sb("gz", [P, HALVES, TOK])
        decay = sb("decay", [P, DECAY_RING, TOK])
        state = sb("state", [P, SCAN_RING, TOK])
        c_all = sb("c_all", [P, C_RING, TOK])
        prod = sb("prod", [P, HALVES, TOK])
        ysum = sb("ysum", [P, 2, HALVES, TOK])
        xtok = sb("xtok", [P, NT, D])
        ctxs = sb("ctxs", [P, TOK])
        x1 = sb("x1", [P, NT, D])
        x1t = sb("x1t", [P, TOK])
        qm = sb("qm", [P, 4, TOK // 2])
        km = sb("km", [P, 4, TOK])
        vv = sb("vv", [P, NB * 8, 2 * (DH + 1)])
        probs = sb("probs", [P, 2, HEADS * SEQ])
        probs_t = sb("probs_t", [P, 8, P])
        att = sb("att", [P, NT, D])
        mx = sb("mx", [P, 2, 8])
        rden = sb("rden", [P, HEADS])
        x2 = sb("x2", [P, NT, D])
        ln_st = sb("ln_st", [P, 3, NT, 6])
        ln_mean = sb("ln_mean", [P, 3, NT])
        ln_tmp = sb("ln_tmp", [P, 2, NT])
        ln_ve = sb("ln_ve", [P, 3, NT])
        ln_rs = sb("ln_rs", [P, 3, NT])
        x2t = sb("x2t", [P, TOK])
        x2t_hi = sb("x2t_hi", [P, TOK], F32R)
        x2t_lo = sb("x2t_lo", [P, TOK], F32R)
        hid = sb("hid", [P, HID_RING, TOK])
        acc = sb("acc", [P, 2, NT, D])
        rl = sb("rl", [P, 4, NT, NEXP])
        rm = sb("rm", [P, 6, NT])
        comb = sb("comb", [P, NT, NEXP])
        ones_row = x2t[0:1, 0:P]

        def pc(name, a=0, b=None, rows=P, row0=0):
            lo, hi = COLS[name]
            return par[row0:row0 + rows, lo + a:(hi if b is None else lo + b)]

        ident = pc("ident")

        b_ps, c_ps, f_ps, y_ps = pb("b_ps"), pb("c_ps"), pb("f_ps"), pb("y_ps")
        h_ps = [pb("h_ps0"), pb("h_ps1")]
        a_ps = [pb("a_ps0"), pb("a_ps1")]

        par_in, w1_in, w2_in = sem("par_in"), sem("w1_in"), sem("w2_in")
        xt_in, ctx_in, xtok_in, stored = sem("xt_in"), sem("ctx_in"), sem("xtok_in"), sem("stored")
        setup = {n: sem("setup_" + n) for n in ("dve", "act", "pe", "pool")}
        xproj_done = sem("f_ps_filled")
        x_in_done = sem("x_in_copied")
        conv_done = sem("conv_step")
        silu_done = sem("silu_done")
        dtlow_done = sem("dt_low_copied")
        split_done = sem("bc_split_step")
        sp_parts = sem("softplus_parts")
        sp_exp = sem("softplus_exp")
        sp_ln = sem("softplus_ln")
        dt_done = sem("dt_done")
        du_done = sem("du_done")
        b_ready = sem("b_ready")
        c_ready = sem("c_ps_filled")
        c_taken = sem("c_ps_taken")
        z_filled = sem("z_filled")
        z_step = sem("z_step")
        decay_done = sem("decay_done")
        input_done = sem("scan_input_done")
        scan_done = sem("scan_done")
        prod_done = sem("prod_done")
        add_done = sem("product_added")
        gate_step = sem("gate_step")
        a_filled = sem("a_ps_filled")
        k_done, v_done, x1t_done = sem("k_done"), sem("v_done"), sem("x1t_done")
        q_done = sem("q_done")
        max_done = sem("max_done")
        shift_done = sem("shift_done")
        exp_done = sem("exp_done")
        pt_done = sem("probs_t_done")
        rden_done = sem("rden_done")
        pv_filled = sem("pv_filled")
        att_done = sem("att_done")
        att_t_done = sem("att_t_done")
        ln_step = [sem(f"ln{i + 1}_step") for i in range(3)]
        ln_rstd = [sem(f"ln{i + 1}_rstd") for i in range(3)]
        ln_out = [sem(f"ln{i + 1}_out") for i in range(3)]
        x1_biased = sem("x1_biased")
        x2t_done = sem("x2t_done")
        x2t_hi_done, x2t_lo_done = sem("x2t_hi_done"), sem("x2t_lo_done")
        h_ready = sem("hidden_ps_ready")
        gelu_done = sem("gelu_done")
        y_filled = sem("y_ps_filled")
        route_step = sem("route_step")
        route_exp = sem("route_exp")
        combt_done = sem("comb_t_done")
        acc_done = sem("acc_done")

        def at(chunk, per, k):
            v = chunk * per + k
            return max(v, 0) if isinstance(v, int) else v

        acc_order = ["e0", "e1", "b2"] + [f"e{e}" for e in range(2, NEXP)]

        LN_STEPS = [NT + 8, NT + 8, NT + 7]
        A_READ = {"k": (k_done, 4, 4), "v0": (v_done, 4, 2), "v1": (v_done, 4, 4), "out": (ln_step[0], LN_STEPS[0], 1),
                  "x1t": (x1t_done, 1, 1), "q0": (q_done, 8, 4), "q1": (q_done, 8, 8),
                  "att": (att_t_done, 1, 1), "o": (ln_step[1], LN_STEPS[1], 1)}
        for t in range(NT):
            for u in range(2):
                A_READ[f"sc{t}{u}"] = (shift_done, 8, 2 * t + u + 1)
                A_READ[f"pt{t}{u}"] = (pt_done, 8, 2 * t + u + 1)
        Y_READ = {"x2t": (x2t_done, 1, 1), "router": (route_step, 19, 1), "comb": (combt_done, 1, 1)}
        for name in acc_order:
            Y_READ[name] = (acc_done, 9, acc_order.index(name) + 1)

        def a_before(name):
            i = A_ORDER.index(name)
            return A_ORDER[i - 2 if i >= 2 else max(j for j in range(NA) if j % 2 == i)]

        def a_reader(name):
            return A_READ[a_before(name)][0]

        def a_read(c, name):
            _, per, k = A_READ[a_before(name)]
            return at(c, per, k if A_ORDER.index(name) >= 2 else k - per)

        def a_count(c, name):
            return at(c, NA, A_ORDER.index(name) + 1)

        def a_bank(name):
            return a_ps[A_ORDER.index(name) % 2]

        def y_reader(name):
            return Y_READ[Y_ORDER[Y_ORDER.index(name) - 1]][0]

        def y_read(c, name):
            i = Y_ORDER.index(name)
            _, per, k = Y_READ[Y_ORDER[i - 1]]
            return at(c, per, k if i else k - per)

        def y_count(c, name):
            return at(c, NY, Y_ORDER.index(name) + 1)

        def run(eng, iteration):
            first, last = max(START.values()), CHUNKS
            for it in range(first):
                iteration(it, it % 2)
            with eng.Fori(first, last, 2) as it:
                iteration(it, 0)
                iteration(it + 1, 1)
            for it in range(last, CHUNKS + max(START.values())):
                iteration(it, it % 2)

        def chunks_of(it):
            return {s: it - b for s, b in START.items()
                    if not isinstance(it, int) or 0 <= it - b < CHUNKS}

        SETUP_DVE = 13

        block = ctx.enter_context(nc.Block())

        @block.sync
        def _(sp):
            sp.dma_start(par[:], params).then_inc(par_in, 16)
            sp.dma_start(xt[:, 0, :], x_t[0]).then_inc(xt_in, 16)
            sp.dma_start(ctxs[:], ctx_t[0]).then_inc(ctx_in, 16)
            sp.dma_start(xtok[:], x_tok[0]).then_inc(xtok_in, 16)
            sp.dma_start(hid[:].rearrange("p u t -> p (u t)"), w1).then_inc(w1_in, 16)
            sp.dma_start(w2s[:], w2).then_inc(w2_in, 16)

            def iteration(it, p):
                c = chunks_of(it)
                if "F" in c and not (isinstance(it, int) and it + 1 >= CHUNKS):
                    if "S" in c:
                        sp.wait_ge(z_filled, at(c["S"], 2, 2))
                    else:
                        sp.wait_ge(xt_in, 16)
                    sp.dma_start(xt[:, 1 - p, :], x_t[it + 1]).then_inc(xt_in, 16)
                if "O" in c:
                    sp.wait_ge(ln_out[2], at(c["O"], 4, 4))
                    sp.dma_start(out[c["O"]], acc[:, p]).then_inc(stored, 16)
                if "A" in c and not (isinstance(it, int) and c["A"] + 1 >= CHUNKS):
                    sp.wait_ge(a_filled, a_count(c["A"], "v1"))
                    sp.dma_start(ctxs[:], ctx_t[c["A"] + 1]).then_inc(ctx_in, 16)
                    sp.wait_ge(ln_step[0], at(c["A"], LN_STEPS[0], 1))
                    sp.dma_start(xtok[:], x_tok[c["A"] + 1]).then_inc(xtok_in, 16)

            first, last = max(START.values()), CHUNKS
            for it in range(first):
                iteration(it, it % 2)
            with sp.Fori(first, last - 2, 2) as it:
                iteration(it, 0)
                iteration(it + 1, 1)
            for it in range(last - 2, CHUNKS + max(START.values())):
                iteration(it, it % 2)
            sp.wait_ge(stored, 16 * CHUNKS)

        @block.tensor
        def _(pe):
            pe.wait_ge(par_in, 16)
            pe.wait_ge(setup["dve"], 2)
            pe.matmul(f_ps[:, 0:D], pc("bv").to_broadcast([P, P]), pc("wo"), start=True, stop=False)
            pe.matmul(f_ps[:, 0:D], ones_row, pc("bo_row", rows=1), start=False, stop=True)\
                .then_inc(setup["pe"], 1)
            pe.wait_ge(setup["act"], 2)

            def hidden(c, units):
                for u in units:
                    pe.wait_ge(gelu_done, at(c, HID_UNITS, u - 1))
                    w_hi, w_lo = w1_hi[:, u * P:(u + 1) * P], w1_lo[:, u * P:(u + 1) * P]
                    pe.matmul(h_ps[u % 2][:], w_hi, x2t_hi[:], start=True, stop=False)
                    pe.matmul(h_ps[u % 2][:], w_lo, x2t_hi[:], start=False, stop=False)
                    if u == 0:
                        pe.wait_ge(x2t_lo_done, at(c, 1, 1))
                    pe.matmul(h_ps[u % 2][:], w_hi, x2t_lo[:], start=False, stop=True).then_inc(h_ready, 1)

            def project(c, e):
                name = f"e{e}"
                pe.wait_ge(y_reader(name), y_read(c, name))
                pe.wait_ge(gelu_done, at(c, HID_UNITS, HB4 * (e + 1)))
                for t in range(NT):
                    for j in range(HB4):
                        u = HB4 * e + j
                        mm = pe.matmul(y_ps[:, t * P:(t + 1) * P], hid[:, u % HID_RING, t * P:(t + 1) * P],
                                       w2s[:, u * D:(u + 1) * D], start=j == 0, stop=j == HB4 - 1)
                mm.then_inc(y_filled, 1)

            def scores(c, t):
                pe.wait_ge(q_done, at(c, 8, 4 * (t // 2) + 4))
                if t == 0:
                    pe.wait_ge(k_done, at(c, 4, 4))
                for u in range(2):
                    name = f"sc{t}{u}"
                    pe.wait_ge(a_reader(name), a_read(c, name))
                    for g in range(2):
                        for s in range(2):
                            q = qm[:, 2 * u + g, (t % 2) * P + s * SEQ:(t % 2) * P + (s + 1) * SEQ]
                            k = km[:, :, t * P + s * SEQ:t * P + (s + 1) * SEQ]
                            mm = pe.matmul(a_bank(name)[s * SEQ:(s + 1) * SEQ, g * 256:(g + 1) * 256],
                                           q, k, start=True, stop=True)
                    mm.then_inc(a_filled, 1)

            def probs_transposed(c, t):
                pe.wait_ge(exp_done, at(c, NT, t + 1))
                for u in range(2):
                    name = f"pt{t}{u}"
                    pe.wait_ge(a_reader(name), a_read(c, name))
                    for k in range(4):
                        hp = 4 * u + k
                        mm = pe.transpose(a_bank(name)[:, k * P:(k + 1) * P],
                                          probs[:, t % 2, hp * P:(hp + 1) * P], ident)
                    mm.then_inc(a_filled, 1)

            def values(c, t):
                pe.wait_ge(pt_done, at(c, 8, 2 * t + 2))
                if t:
                    pe.wait_ge(att_done, at(c, 4, t))
                if t == 0:
                    pe.wait_ge(v_done, at(c, 4, 4))
                for hp in range(8):
                    for s in range(2):
                        mm = pe.matmul(f_ps[s * SEQ:(s + 1) * SEQ, hp * 18:(hp + 1) * 18],
                                       probs_t[:, hp, s * SEQ:(s + 1) * SEQ], vv[:, (2 * t + s) * 8 + hp, :],
                                       start=True, stop=True)
                mm.then_inc(pv_filled, 1)

            def q_proj(c, half):
                name = f"q{half}"
                pe.wait_ge(a_reader(name), a_read(c, name))
                if half == 0:
                    pe.wait_ge(x1t_done, at(c, 1, 1))
                pe.matmul(a_bank(name)[:, 0:256], pc("wq"), x1t[:, half * 256:(half + 1) * 256],
                          start=True, stop=True).then_inc(a_filled, 1)

            def v_proj(c, v):
                name = f"v{v}"
                pe.wait_ge(a_reader(name), a_read(c, name))
                for k in range(4):
                    b = 4 * v + k
                    for r in range(2):
                        mm = pe.matmul(a_bank(name)[r * SEQ:(r + 1) * SEQ, k * P:(k + 1) * P],
                                       ctxs[:, b * SEQ:(b + 1) * SEQ], pc("wv"), start=True, stop=True)
                mm.then_inc(a_filled, 1)

            def dt_proj(F, h):
                if h == 0:
                    pe.wait_ge(split_done, at(F, 5, 2))
                    pe.wait_ge(dtlow_done, at(F, 1, 1))
                else:
                    pe.wait_ge(sp_parts, at(F, 4, 2))
                pe.matmul(f_ps[:], pc("w_dt_rows", h * P, (h + 1) * P, DTR, 96),
                          dt_low, start=True, stop=True).then_inc(xproj_done, 1)

            def broadcast_b(S, q, n):
                if n == 0:
                    pe.wait_ge(split_done, at(S, 5, 5))
                pe.wait_ge(input_done, at(S, UNITS, 2 * n))
                pe.matmul(b_ps[:], select_bf[:, n:n + 1].to_broadcast([96, P]), bc3[:, q, :],
                          start=True, stop=True).then_inc(b_ready, 1)

            def broadcast_c(S, q, n):
                pe.wait_ge(c_taken, at(S, NSTATE, n))
                pe.matmul(c_ps[:], select_bf[:, NSTATE + n:NSTATE + n + 1].to_broadcast([96, P]),
                          bc3[:, q, :], start=True, stop=True).then_inc(c_ready, 1)

            def z_half(S, p, h):
                lo = E_IN + h * P
                pe.matmul(f_ps[:], pc("w_in", lo, lo + P), xt[:, 1 - p, :], start=True, stop=True)\
                    .then_inc(z_filled, 1)

            def x_half(F, p, h):
                pe.matmul(f_ps[:], pc("w_in", h * P, (h + 1) * P), xt[:, p, :], start=True, stop=True)\
                    .then_inc(xproj_done, 1)

            def iteration(it, p):
                c = chunks_of(it)
                F, S, A, M = (c.get(x) for x in "FSAM")
                if isinstance(it, int) and it == START["M"]:
                    pe.wait_ge(setup["dve"], SETUP_DVE)
                    pe.wait_ge(w2_in, 16)
                for s in range(SLOTS):
                    if S is not None and s in EARLY_B:
                        broadcast_b(S, 1 - p, s + 1)
                    if S is not None and s in EARLY_C:
                        broadcast_c(S, 1 - p, s + 1)
                    if F is not None and s == 0:
                        pe.wait_ge(xt_in, at(F, 16, 16))
                        pe.wait_ge(sp_parts, at(F, 4, 0))
                        pe.wait_ge(att_done, at(F - 2, 4, 0))
                        x_half(F, p, 0)
                    if A is not None:
                        if s == 3:
                            v_proj(A, 0)
                        if s == 14:
                            pe.wait_ge(a_reader("att"), a_read(A, "att"))
                            pe.wait_ge(att_done, at(A, 4, 4))
                            for t in range(NT):
                                mm = pe.transpose(a_bank("att")[:, t * P:(t + 1) * P], att[:, t, :], ident)
                            mm.then_inc(a_filled, 1)
                        if s == 15:
                            pe.wait_ge(a_reader("o"), a_read(A, "o"))
                            pe.wait_ge(att_t_done, at(A, 1, 1))
                            for t in range(NT):
                                mm = pe.matmul(a_bank("o")[:, t * P:(t + 1) * P], x1t[:, t * P:(t + 1) * P],
                                               pc("wo"), start=True, stop=True)
                            mm.then_inc(a_filled, 1)
                    if S is not None and s == 2:
                        if F is not None:
                            pe.wait_ge(x_in_done, at(F, 2, 2))
                        else:
                            pe.wait_ge(att_done, at(S - 1, 4, 0))
                        z_half(S, p, 0)
                    if M is not None:
                        if s in HIDDEN_SLOTS and s not in (0, 5):
                            hidden(M, range(HIDDEN_SLOTS[s], HIDDEN_SLOTS[s] + 2))
                        if s == 6:
                            pe.wait_ge(y_reader("b2"), y_read(M, "b2"))
                            pe.wait_ge(combt_done, at(M, 1, 1))
                            for t in range(NT):
                                mm = pe.matmul(y_ps[:, t * P:(t + 1) * P], comb_t[:, t * P:(t + 1) * P],
                                               pc("b2_rows", rows=NEXP), start=True, stop=True)
                            mm.then_inc(y_filled, 1)
                        if s in (10, 11, 14):
                            project(M, PROJECT_SLOTS[s])
                    if S is not None and s < SLOTS - 1:
                        if s not in EARLY_B:
                            broadcast_b(S, 1 - p, s + 1)
                        if s not in EARLY_C:
                            broadcast_c(S, 1 - p, s + 1)
                    if F is not None and s == SLOTS - 1:
                        broadcast_b(F, p, 0)
                        broadcast_c(F, p, 0)
                    if A is not None:
                        if s == 5:
                            scores(A, 0)
                        if s == 1:
                            pe.wait_ge(a_reader("out"), a_read(A, "out"))
                            pe.wait_ge(gate_step, at(A, 4, 4))
                            for t in range(NT):
                                for h in range(HALVES):
                                    mm = pe.matmul(a_bank("out")[:, t * P:(t + 1) * P],
                                                   gz[:, h, t * P:(t + 1) * P],
                                                   pc("w_out", h * D, (h + 1) * D), start=h == 0, stop=h == 1)
                            mm.then_inc(a_filled, 1)
                        if s == 4:
                            q_proj(A, 0)
                            v_proj(A, 1)
                        if s == 6:
                            scores(A, 1)
                        if s == 8:
                            scores(A, 2)
                        if s == 9:
                            if F is not None:
                                pe.wait_ge(sp_parts, at(F, 4, 4))
                            if F is None and S is not None:
                                pe.wait_ge(z_step, at(S, 4, 2))
                            if F is None and S is None:
                                pe.wait_ge(att_done, at(A, 4, 0))
                            values(A, 0)
                        if s == 11:
                            probs_transposed(A, 2)
                        if s == 12:
                            values(A, 2)
                            probs_transposed(A, 3)
                        if s == 13:
                            values(A, 3)
                        if s == 7:
                            q_proj(A, 1)
                    if F is not None and s == 6:
                        if S is not None:
                            pe.wait_ge(z_step, at(S, 4, 2))
                        for h in range(HALVES):
                            pe.wait_ge(silu_done, at(F, 2, h + 1))
                            mm = pe.matmul(f_ps[0:104, :], pc("w_xp", h * 104, (h + 1) * 104),
                                           xc[:, p, h, :], start=h == 0, stop=h == 1)
                        mm.then_inc(xproj_done, 1)
                    if M is not None:
                        if s == 0:
                            pe.wait_ge(y_reader("x2t"), y_read(M, "x2t"))
                            for t in range(NT):
                                pe.wait_ge(ln_out[1], at(M, 4, t + 1))
                                mm = pe.transpose(y_ps[:, t * P:(t + 1) * P], x2[:, t, :], ident)
                            mm.then_inc(y_filled, 1)
                    if F is not None and s == 0:
                        pe.wait_ge(x_in_done, at(F, 2, 1))
                        x_half(F, p, 1)
                    if A is not None and s == 0:
                        pe.wait_ge(ctx_in, at(A, 16, 16))
                        pe.wait_ge(a_reader("k"), a_read(A, "k"))
                        pe.matmul(a_bank("k")[:], pc("wk"), ctxs[:], start=True, stop=True)\
                            .then_inc(a_filled, 1)
                    if M is not None:
                        if s == 0:
                            pe.wait_ge(x2t_done, at(M, 1, 1))
                            pe.wait_ge(x2t_hi_done, at(M, 1, 1))
                            for t in range(NT):
                                mm = pe.matmul(y_ps[:, t * NEXP:(t + 1) * NEXP], x2t[:, t * P:(t + 1) * P],
                                               pc("router"), start=True, stop=True)
                            mm.then_inc(y_filled, 1)
                        if s in (0, 5):
                            hidden(M, range(HIDDEN_SLOTS[s], HIDDEN_SLOTS[s] + 2))
                        if s == 5:
                            pe.wait_ge(y_reader("comb"), y_read(M, "comb"))
                            pe.wait_ge(route_step, at(M, 19, 19))
                            for t in range(NT):
                                mm = pe.transpose(y_ps[0:NEXP, t * P:(t + 1) * P], comb[:, t, :], ident)
                            mm.then_inc(y_filled, 1)
                        if s in HIDDEN_SLOTS:
                            hidden(M, range(HIDDEN_SLOTS[s] + 2, HIDDEN_SLOTS[s] + 4))
                        if s in PROJECT_SLOTS and s not in (10, 11, 14):
                            project(M, PROJECT_SLOTS[s])
                    if A is not None:
                        if s == 3:
                            pe.wait_ge(a_reader("x1t"), a_read(A, "x1t"))
                            for t in range(NT):
                                pe.wait_ge(ln_out[0], at(A, 4, t + 1))
                                mm = pe.transpose(a_bank("x1t")[:, t * P:(t + 1) * P], x1[:, t, :], ident)
                            mm.then_inc(a_filled, 1)
                    if F is not None and s in (7, 8):
                        dt_proj(F, s - 7)
                    if A is not None:
                        if s == 7:
                            probs_transposed(A, 0)
                        if s == 9:
                            probs_transposed(A, 1)
                        if s == 10:
                            scores(A, 3)
                            values(A, 1)
                    if S is not None and s == 4:
                        pe.wait_ge(z_step, at(S, 4, 1))
                        z_half(S, p, 1)

            pe.wait_ge(setup["dve"], SETUP_DVE - 2)
            run(pe, iteration)

        @block.scalar
        def _(act):
            act.wait_ge(par_in, 16)
            act.activation(neg_a[:], pc("a_log"), ACT.Exp).then_inc(setup["act"], 1)
            act.wait_ge(setup["pe"], 1)
            act.activation(bo[:], f_ps[:, 0:D], ACT.Copy).then_inc(setup["act"], 1)
            act.wait_ge(setup["dve"], SETUP_DVE - 2)

            def per_seq(ap):
                return ap.rearrange("p (b t) -> p b t", b=NB)

            def decays(S, p, n):
                for h in range(HALVES):
                    u = 2 * n + h
                    act.wait_ge(scan_done, at(S, UNITS, u - DECAY_RING + 1))
                    if u == 0:
                        act.wait_ge(dt_done, at(S, 2, 2))
                    act.activation(per_seq(decay[:, u % DECAY_RING, :])[:, :, 1:],
                                   per_seq(dt[:, p, h, :])[:, :, 1:], ACT.Exp,
                                   scale=neg_a[:, h * NSTATE + n:h * NSTATE + n + 1]).then_inc(decay_done, 1)

            def gelus(M, units):
                for u in units:
                    act.wait_ge(h_ready, at(M, HID_UNITS, u + 1))
                    if u % HB4 == 0:
                        e = u // HB4 - 2
                        k = Y_ORDER.index(f"e{e}") + 1 if e >= 0 else Y_ORDER.index(f"e{e + NEXP}") + 1 - NY
                        act.wait_ge(y_filled, at(M, NY, k))
                    act.activation(hid[:, u % HID_RING, :], h_ps[u % 2][:], ACT.Gelu_apprx_tanh,
                                   bias=pc("b1", u, u + 1)).then_inc(gelu_done, 1)

            def q_parts(A, half):
                act.wait_ge(a_filled, a_count(A, f"q{half}"))
                for g in range(4):
                    act.activation(qm[:, g, :], a_bank(f"q{half}")[:, 0:256], ACT.Identity,
                                   scale=qscale[:, 2 * g:2 * g + 1], bias=qscale[:, 2 * g + 1:2 * g + 2])\
                        .then_inc(q_done, 1)


            def exp_probs(A, t):
                act.wait_ge(shift_done, at(A, 8, 2 * t + 2))
                act.activation(probs[:, t % 2, :], probs[:, t % 2, :], ACT.Exp).then_inc(exp_done, 1)

            def pt_copies(A, t):
                for u in range(2):
                    name = f"pt{t}{u}"
                    act.wait_ge(a_filled, a_count(A, name))
                    act.activation(probs_t[:, 4 * u:4 * u + 4, :], a_bank(name)[:].rearrange("p (k q) -> p k q", k=4),
                                   ACT.Copy).then_inc(pt_done, 1)

            def v_parts(A, v):
                act.wait_ge(a_filled, a_count(A, f"v{v}"))
                src = a_bank(f"v{v}")[:].rearrange("p (b k r d) -> p (b k) r d", b=4, k=8, r=2)
                dst = vv[:, 32 * v:32 * v + 32, :].rearrange("p k (r d) -> p k r d", r=2)
                for r in range(2):
                    act.activation(dst[:, :, r, 0:DH], src[:, :, r, :], ACT.Copy,
                                   scale=pc("half_mask", r, r + 1)).then_inc(v_done, 1)

            def x_copy(F, p, h):
                act.wait_ge(xproj_done, at(F, NF, h + 1))
                act.activation(du[:, p, h, :], f_ps[:], ACT.Copy).then_inc(x_in_done, 1)

            def copy_c(S, n):
                act.wait_ge(c_ready, at(S, NSTATE, n + 1))
                act.wait_ge(prod_done, at(S, UNITS, 2 * (n + 1 - C_RING)))
                act.activation(c_all[:, n % C_RING, :], c_ps[:], ACT.Copy).then_inc(c_taken, 1)

            def softplus_parts(F, p, h):
                act.wait_ge(xproj_done, at(F, NF, 4 + h))
                if h == 0:
                    act.wait_ge(split_done, at(F, 5, 5))
                act.activation(dt[:, p, h, :], f_ps[:], ACT.Relu, bias=pc("b_dt", h, h + 1)).then_inc(sp_parts, 1)
                act.activation(du[:, p, h, :], f_ps[:], ACT.Abs, bias=pc("b_dt", h, h + 1)).then_inc(sp_parts, 1)

            def iteration(it, p):
                c = chunks_of(it)
                F, S, A, M = (c.get(x) for x in "FSAM")

                def next_c(s):
                    if S is not None and s < SLOTS - 1:
                        copy_c(S, s + 1)
                    if F is not None and s == SLOTS - 1:
                        copy_c(F, 0)

                if isinstance(it, int) and it == START["M"]:
                    act.wait_ge(setup["dve"], SETUP_DVE)
                for s in range(SLOTS):
                    if M is not None and s == 2:
                        act.wait_ge(route_step, at(M, 19, 13))
                        act.activation(rm[:, 3, :], rm[:, 2, :], ACT.Exp).then_inc(route_exp, 1)
                    if A is not None:
                        if s == 2:
                            act.wait_ge(a_filled, a_count(A, "k"))
                            for j in range(4):
                                act.activation(km[:, j, :], a_bank("k")[:], ACT.Identity,
                                               scale=pc("head_mask", j, j + 1), bias=kbias[:, j:j + 1])\
                                    .then_inc(k_done, 1)
                        if s == 10:
                            pt_copies(A, 1)
                    if s == 2:
                        next_c(s)
                    if S is not None:
                        if s == 6:
                            for h in range(HALVES):
                                act.wait_ge(z_step, at(S, 4, h + 1))
                                act.activation(gz[:, h, :], gz[:, h, :], ACT.Silu).then_inc(z_step, 1)
                        for n in DECAY_SLOTS.get(s, []):
                            decays(S, 1 - p, n)
                    if A is not None and s == 14:
                        act.wait_ge(a_filled, a_count(A, "att"))
                        act.activation(x1t[:], a_bank("att")[:], ACT.Copy).then_inc(att_t_done, 1)
                    if s in (3, 6, 7, 10, 11, 14):
                        next_c(s)
                    if S is not None:
                        if s == 3:
                            act.wait_ge(z_filled, at(S, 2, 1))
                            act.wait_ge(a_filled, a_count(S - 1, "out"))
                            act.activation(gz[:, 0, :], f_ps[:], ACT.Copy).then_inc(z_step, 1)
                        if s == 5:
                            act.wait_ge(z_filled, at(S, 2, 2))
                            act.activation(gz[:, 1, :], f_ps[:], ACT.Copy).then_inc(z_step, 1)
                    if M is not None and s == 0:
                        act.activation(warm[:], ones[:], ACT.Gelu_apprx_tanh)
                    if F is not None:
                        if s == 0:
                            act.wait_ge(input_done, at(F - 1, UNITS, 0))
                            x_copy(F, p, 0)
                        if s == 6:
                            act.wait_ge(xproj_done, at(F, NF, 3))
                            act.activation(dt_low, f_ps[96:96 + DTR, :], ACT.Copy).then_inc(dtlow_done, 1)
                        if s in (8, 9):
                            softplus_parts(F, p, s - 8)
                    if M is not None and s == 0:
                        act.wait_ge(y_filled, y_count(M, "x2t"))
                        act.wait_ge(h_ready, at(M, HID_UNITS, 0))
                        act.activation(x2t_hi[:], y_ps[:], ACT.Copy).then_inc(x2t_hi_done, 1)
                        act.activation(x2t[:], y_ps[:], ACT.Copy).then_inc(x2t_done, 1)
                    if F is not None and s == 0:
                        x_copy(F, p, 1)
                    if A is not None:
                        if s == 4:
                            act.wait_ge(a_filled, a_count(A, "x1t"))
                            act.activation(x1t[:], a_bank("x1t")[:], ACT.Copy).then_inc(x1t_done, 1)
                            v_parts(A, 0)
                        if s == 8:
                            pt_copies(A, 0)
                    if s in (0, 5):
                        next_c(s)
                    if M is not None and s in HIDDEN_SLOTS:
                        gelus(M, range(HIDDEN_SLOTS[s], HIDDEN_SLOTS[s] + 2))
                    if s in (1, 4, 8, 9, 12, 13):
                        next_c(s)
                    if M is not None and s in HIDDEN_SLOTS:
                        if s == 4 and A is not None:
                            q_parts(A, 0)
                            v_parts(A, 1)
                        if s == 5:
                            act.wait_ge(y_filled, y_count(M, "comb"))
                            act.activation(comb_t, y_ps[0:NEXP, :], ACT.Copy).then_inc(combt_done, 1)
                        gelus(M, range(HIDDEN_SLOTS[s] + 2, HIDDEN_SLOTS[s] + 4))
                    if A is not None:
                        if s == 4 and M is None:
                            q_parts(A, 0)
                            v_parts(A, 1)
                        if s == 6:
                            exp_probs(A, 0)
                        if s == 7:
                            q_parts(A, 1)
                            exp_probs(A, 1)
                        if s == 10:
                            exp_probs(A, 2)
                        if s == 11:
                            exp_probs(A, 3)
                        if s == 12:
                            pt_copies(A, 3)
                    if F is not None:
                        if s == 5:
                            for h in range(HALVES):
                                act.wait_ge(conv_done, at(F, 8, 7 + h))
                                act.activation(xc[:, p, h, :], xc[:, p, h, :], ACT.Silu).then_inc(silu_done, 1)
                        if s == 10:
                            for h in range(HALVES):
                                act.wait_ge(sp_parts, at(F, 4, 2 * h + 2))
                                act.activation(du[:, p, h, :], du[:, p, h, :], ACT.Exp, scale=-1.0)\
                                    .then_inc(sp_exp, 1)
                        if s == 11:
                            for h in range(HALVES):
                                act.wait_ge(sp_exp, at(F, 2, h + 1))
                                act.activation(du[:, p, h, :], du[:, p, h, :], ACT.Ln, bias=1.0).then_inc(sp_ln, 1)
                        for n in FIRST_DECAYS.get(s, []):
                            decays(F, p, n)
                    if s == 15:
                        next_c(s)

            run(act, iteration)

        @block.vector
        def _(dve):
            dve.memset(decay[:], 0.0).then_inc(setup["dve"], 1)
            dve.memset(ones_row, 1.0).then_inc(setup["dve"], 1)
            dve.memset(ones[:], 1.0).then_inc(setup["dve"], 1)
            dve.memset(vv[:], 0.0).then_inc(setup["dve"], 1)
            dve.wait_ge(par_in, 16)
            dve.tensor_copy(select_bf[:], pc("select", rows=96)).then_inc(setup["dve"], 1)
            dve.tensor_scalar(kbias[:], pc("head_mask"), pc("bk"), None, ALU.mult).then_inc(setup["dve"], 1)
            dve.wait_ge(setup["dve"], 4)
            for r in range(2):
                one = vv[:, :, r * (DH + 1) + DH]
                dve.tensor_scalar(one, one, pc("half_mask", r, r + 1), None,
                                  ALU.add).then_inc(setup["dve"], 1)
            qv = qscale[:].rearrange("p (g k) -> p g k", k=2)
            dve.tensor_scalar(qv[:, :, 0], pc("group_mask"), float(DH) ** -0.5, None, ALU.mult)\
                .then_inc(setup["dve"], 1)
            dve.tensor_scalar(qv[:, :, 1], pc("group_mask"), pc("bq"), float(DH) ** -0.5, ALU.mult, ALU.mult)\
                .then_inc(setup["dve"], 1)
            dve.wait_ge(setup["act"], 1)
            dve.tensor_scalar(neg_a[:], neg_a[:], -1.0, None, ALU.mult).then_inc(setup["dve"], 1)

            def ln_stats(c, i, src, made, made_at):
                for t in range(NT):
                    if t == 0:
                        dve.wait_ge(made, made_at)
                    dve.bn_stats(ln_st[:, i, t, :], src[:, t, :]).then_inc(ln_step[i], 1)
                st, a, b = ln_st[:, i], ln_tmp[:, 0], ln_tmp[:, 1]
                mean, ve = ln_mean[:, i, :], ln_ve[:, i, :]

                def step(n, after, op, *args):
                    dve.wait_ge(ln_step[i], at(c, LN_STEPS[i], LN_STEPS[i] - 7 + after))
                    op(*args).then_inc(ln_step[i], 1)

                step(1, 0, dve.tensor_tensor, mean, st[:, :, 1], st[:, :, 4], ALU.add)
                step(2, 0, dve.tensor_tensor, a, st[:, :, 1], st[:, :, 4], ALU.subtract)
                step(3, 0, dve.tensor_tensor, b, st[:, :, 2], st[:, :, 5], ALU.add)
                step(4, 1, dve.tensor_scalar, mean, mean, 0.5, None, ALU.mult)
                step(5, 2, dve.scalar_tensor_tensor, a, a, 0.25, a, ALU.mult, ALU.mult)
                step(6, 5, dve.scalar_tensor_tensor, ve, b, 1.0 / D, a, ALU.mult, ALU.add)
                step(7, 6, dve.tensor_scalar, ve, ve, EPS, None, ALU.add)

            def ln_scale(c, i, dst, src):
                dve.wait_ge(ln_rstd[i], at(c, 1, 1))
                for t in range(NT):
                    dve.tensor_scalar(dst[:, t, :], src[:, t, :], ln_mean[:, i, t:t + 1], ln_rs[:, i, t:t + 1],
                                      ALU.subtract, ALU.mult).then_inc(ln_out[i], 1)

            def conv_taps(F, p, taps):
                for i, k in taps:
                    sh = NCONV - 1 - k
                    for h in range(HALVES):
                        w = pc("conv_w", h * NCONV + k, h * NCONV + k + 1)
                        if i == 0:
                            dve.wait_ge(x_in_done, at(F, 2, h + 1))
                            dve.tensor_scalar(xc[:, p, h, :], du[:, p, h, :], w, pc("conv_b", h, h + 1),
                                              ALU.mult, ALU.add).then_inc(conv_done, 1)
                        else:
                            dve.wait_ge(conv_done, at(F, 8, 2 * i + h - 1))
                            o = xc[:, p, h, :].rearrange("p (b t) -> p b t", b=NB)[:, :, sh:]
                            a = du[:, p, h, :].rearrange("p (b t) -> p b t", b=NB)[:, :, 0:SEQ - sh]
                            dve.scalar_tensor_tensor(o, a, w, o, ALU.mult, ALU.add).then_inc(conv_done, 1)

            def shift(A, t):
                for u in range(2):
                    name = f"sc{t}{u}"
                    v = a_bank(name)[:].rearrange("p (h k) -> p h k", h=8)
                    dve.wait_ge(a_filled, a_count(A, name))
                    dve.tensor_reduce(mx[:, u, :], v, AX.X, ALU.max).then_inc(max_done, 1)
                    dve.wait_ge(max_done, at(A, 8, 2 * t + u + 1))
                    dve.tensor_tensor(probs[:, t % 2, u * TOK:(u + 1) * TOK].rearrange("p (h k) -> p h k", h=8), v,
                                      mx[:, u, :].unsqueeze(2).to_broadcast([P, 8, SEQ]), ALU.subtract)\
                        .then_inc(shift_done, 1)


            def normalise(A, t):
                v = f_ps[:, 0:HEADS * (DH + 1)].rearrange("p (h d) -> p h d", h=HEADS)
                dve.wait_ge(pv_filled, at(A, 4, t + 1))
                dve.reciprocal(rden[:], v[:, :, DH]).then_inc(rden_done, 1)
                dve.wait_ge(rden_done, at(A, 4, t + 1))
                dve.tensor_tensor(att[:, t, :].rearrange("p (h d) -> p h d", h=HEADS), v[:, :, 0:DH],
                                  rden[:].unsqueeze(2).to_broadcast([P, HEADS, DH]), ALU.mult).then_inc(att_done, 1)

            def over_experts(i):
                return rm[:, i, :].unsqueeze(2).to_broadcast([P, NT, NEXP])

            def route(M, n, op, *args):
                if n > 1:
                    dve.wait_ge(route_step, at(M, 19, n - 1))
                op(*args).then_inc(route_step, 1)

            def choose_experts(M):
                tie = pc("tie_order").unsqueeze(1).to_broadcast([P, NT, NEXP])
                dve.wait_ge(y_filled, y_count(M, "router"))
                route(M, 1, dve.tensor_copy, rl[:, 0], y_ps[:, 0:NT * NEXP].rearrange("p (t e) -> p t e", t=NT))
                for i in range(2):
                    n = 2 + 6 * i
                    route(M, n, dve.tensor_reduce, rm[:, i, :], rl[:, 0], AX.X, ALU.max)
                    route(M, n + 1, dve.tensor_tensor, rl[:, 3], rl[:, 0], over_experts(i), ALU.is_equal)
                    route(M, n + 2, dve.tensor_tensor, rl[:, 3], rl[:, 3], tie, ALU.mult)
                    route(M, n + 3, dve.tensor_reduce, rm[:, 4, :], rl[:, 3], AX.X, ALU.max)
                    route(M, n + 4, dve.tensor_tensor, rl[:, 1 + i], rl[:, 3], over_experts(4), ALU.is_equal)
                    if i == 0:
                        route(M, 7, dve.scalar_tensor_tensor, rl[:, 0], rl[:, 1], -1e30, rl[:, 0],
                              ALU.mult, ALU.add)
                route(M, 13, dve.tensor_tensor, rm[:, 2, :], rm[:, 1, :], rm[:, 0, :], ALU.subtract)

            def weigh_experts(M):
                dve.wait_ge(route_exp, at(M, 1, 1))
                route(M, 14, dve.tensor_scalar, rm[:, 4, :], rm[:, 3, :], 1.0, None, ALU.add)
                route(M, 15, dve.reciprocal, rm[:, 4, :], rm[:, 4, :])
                route(M, 16, dve.tensor_tensor, rm[:, 5, :], rm[:, 3, :], rm[:, 4, :], ALU.mult)
                route(M, 17, dve.tensor_tensor, rl[:, 1], rl[:, 1], over_experts(4), ALU.mult)
                route(M, 18, dve.tensor_tensor, rl[:, 2], rl[:, 2], over_experts(5), ALU.mult)
                route(M, 19, dve.tensor_tensor, comb[:], rl[:, 1], rl[:, 2], ALU.add)

            def combine(M, q, e):
                dve.wait_ge(y_filled, y_count(M, f"e{e}"))
                if e == 0:
                    dve.wait_ge(route_step, at(M, 19, 19))
                    dve.wait_ge(stored, at(M - 1, 16, 0))
                for t in range(NT):
                    if t == 0 and e:
                        dve.wait_ge(acc_done, at(M, 9, acc_order.index(f"e{e}")))
                    ins = dve.scalar_tensor_tensor(acc[:, q, t, :], y_ps[:, t * P:(t + 1) * P], comb[:, t, e:e + 1],
                                                   (acc[:, q] if e else x2)[:, t, :], ALU.mult, ALU.add)
                ins.then_inc(acc_done, 1)

            def pt_copies(A, t):
                for u in range(2):
                    name = f"pt{t}{u}"
                    dve.wait_ge(a_filled, a_count(A, name))
                    dve.tensor_copy(probs_t[:, 4 * u:4 * u + 4, :],
                                    a_bank(name)[:].rearrange("p (k q) -> p k q", k=4)).then_inc(pt_done, 1)

            def split_w1():
                staged = hid[:].rearrange("p u t -> p (u t)")
                dve.wait_ge(w1_in, 16)
                dve.tensor_copy(w1_hi[:], staged).then_inc(setup["dve"], 1)
                dve.wait_ge(setup["dve"], SETUP_DVE - 1)
                dve.tensor_tensor(w1_lo[:], staged, w1_hi[:].bitcast(F32), ALU.subtract).then_inc(setup["dve"], 1)

            def scans(S, n):
                for h in range(HALVES):
                    u = 2 * n + h
                    dve.wait_ge(decay_done, at(S, UNITS, u + 1))
                    dve.wait_ge(input_done, at(S, UNITS, u + 1))
                    dve.tensor_tensor_scan(state[:, u % SCAN_RING, :], decay[:, u % DECAY_RING, :],
                                           state[:, u % SCAN_RING, :], 0.0, ALU.mult, ALU.add)\
                        .then_inc(scan_done, 1)

            def split_bc(F, p):
                r1 = du[0:96, p, 0, :]
                t2 = du[0:96, p, 1, 0:TOK // 2].bitcast(BF16)
                dve.wait_ge(xproj_done, at(F, NF, 3))
                dve.wait_ge(c_ready, at(F - 1, NSTATE, 0))
                dve.tensor_copy(bc3[:, p, :], f_ps[0:96, :]).then_inc(split_done, 1)
                dve.wait_ge(split_done, at(F, 5, 1))
                dve.tensor_tensor(r1, f_ps[0:96, :], bc3[:, p, :], ALU.subtract).then_inc(split_done, 1)
                dve.wait_ge(split_done, at(F, 5, 2))
                dve.tensor_copy(bc3[32:64, p, :], r1[32:64]).then_inc(split_done, 1)
                dve.tensor_copy(t2[64:96], r1[64:96]).then_inc(split_done, 1)
                dve.wait_ge(split_done, at(F, 5, 4))
                dve.tensor_tensor(bc3[64:96, p, :], r1[64:96], t2[64:96], ALU.subtract).then_inc(split_done, 1)

            def iteration(it, p):
                c = chunks_of(it)
                F, S, A, M, O = (c.get(x) for x in "FSAMO")
                if isinstance(it, int) and it == START["S"]:
                    split_w1()
                for s in range(SLOTS):
                    if S is not None:
                        for h in range(HALVES):
                            u = 2 * s + h
                            if h == 0:
                                if s == 0:
                                    dve.wait_ge(du_done, at(S, 2, 2))
                                dve.wait_ge(b_ready, at(S, NSTATE, s + 1))
                            dve.wait_ge(prod_done, at(S, UNITS, u - SCAN_RING + 1))
                            dve.tensor_tensor(state[:, u % SCAN_RING, :], b_ps[:], du[:, 1 - p, h, :], ALU.mult)\
                                .then_inc(input_done, 1)
                    if S is not None and s in (11, 15):
                        scans(S, s)
                    if O is not None:
                        if s == 0:
                            combine(O, p, NEXP - 1)
                    if M is not None:
                        if s != 7 and s and s - 1 in PROJECT_SLOTS:
                            combine(M, 1 - p, PROJECT_SLOTS[s - 1])
                    if A is not None and s == 12:
                        pt_copies(A, 2)
                    if M is not None and s == 0:
                        ln_scale(M, 1, x2, x2)
                    if A is not None:
                        if s == 3:
                            ln_scale(A, 0, x1, x1)
                        if s in (6, 7, 9):
                            shift(A, (s - 5) // 2)
                        if s == 10:
                            normalise(A, 0)
                        if s in (13, 14):
                            normalise(A, s - 11)
                    if S is not None and s not in (11, 15):
                        scans(S, s)
                    if M is not None:
                        if s == 6:
                            dve.wait_ge(y_filled, y_count(M, "b2"))
                            dve.wait_ge(acc_done, at(M, 9, 2))
                            dve.tensor_tensor(acc[:, 1 - p], y_ps[:].rearrange("p (t d) -> p t d", t=NT),
                                              acc[:, 1 - p], ALU.add).then_inc(acc_done, 1)
                        if s == 7:
                            combine(M, 1 - p, 2)
                    if A is not None and s == 11:
                        shift(A, 3)
                        normalise(A, 1)
                    if F is not None and s == 7:
                        split_bc(F, p)
                    if A is not None and s == 0:
                        for h in range(HALVES):
                            y = ysum[:, p, h, :]
                            dve.wait_ge(add_done, at(A, ADDS, ADDS - 1 + h))
                            dve.scalar_tensor_tensor(y, xc[:, p, h, :], pc("skip_d", h, h + 1), y,
                                                     ALU.mult, ALU.add).then_inc(gate_step, 1)
                        for h in range(HALVES):
                            dve.wait_ge(gate_step, at(A, 4, h + 1))
                            dve.wait_ge(z_step, at(A, 4, h + 3))
                            dve.tensor_tensor(gz[:, h, :], ysum[:, p, h, :], gz[:, h, :], ALU.mult)\
                                .then_inc(gate_step, 1)
                    if M is not None:
                        if s == 1:
                            choose_experts(M)
                    if O is not None:
                        if s == 10:
                            ln_stats(O, 2, acc[:, p], acc_done, at(O, 9, 9))
                        if s == 13:
                            ln_scale(O, 2, acc[:, p], acc[:, p])
                    if A is not None:
                        if s == 2:
                            dve.wait_ge(a_filled, a_count(A, "out"))
                            dve.wait_ge(xtok_in, at(A, 16, 16))
                            dve.tensor_tensor(x1[:], a_bank("out")[:].rearrange("p (t d) -> p t d", t=NT), xtok[:],
                                              ALU.add).then_inc(ln_step[0], 1)
                            ln_stats(A, 0, x1, ln_step[0], at(A, LN_STEPS[0], 1))
                    if M is not None and s == 2:
                        weigh_experts(M)
                    if F is not None:
                        if s == 3:
                            dve.wait_ge(gate_step, at(F - 2, 4, 4))
                            conv_taps(F, p, [(0, 3)])
                        if s == 4:
                            conv_taps(F, p, [(1, 2), (2, 1)])
                        if s == 5:
                            conv_taps(F, p, [(3, 0)])
                    if A is not None:
                        if s == 15:
                            dve.wait_ge(a_filled, a_count(A, "o"))
                            dve.wait_ge(x1_biased, at(A, 1, 1))
                            dve.tensor_tensor(x2[:], a_bank("o")[:].rearrange("p (t d) -> p t d", t=NT), x1[:],
                                              ALU.add).then_inc(ln_step[1], 1)
                            ln_stats(A, 1, x2, ln_step[1], at(A, LN_STEPS[1], 1))
                    if F is not None and s == 13:
                        for h in range(HALVES):
                            dve.wait_ge(sp_ln, at(F, 2, h + 1))
                            dve.tensor_tensor(dt[:, p, h, :], dt[:, p, h, :], du[:, p, h, :], ALU.add)\
                                .then_inc(dt_done, 1)
                        for h in range(HALVES):
                            dve.wait_ge(dt_done, at(F, 2, h + 1))
                            dve.tensor_tensor(du[:, p, h, :], dt[:, p, h, :], xc[:, p, h, :], ALU.mult)\
                                .then_inc(du_done, 1)

            run(dve, iteration)

        @block.gpsimd
        def _(pool):
            pool.memset(half_pow[:], -0.5).then_inc(setup["pool"], 1)
            pool.wait_ge(setup["pool"], 1)
            pool.wait_ge(setup["act"], 2)

            def rstd(c, i):
                pool.wait_ge(ln_step[i], at(c, LN_STEPS[i], LN_STEPS[i]))
                pool.tensor_tensor(ln_rs[:, i, :], ln_ve[:, i, :], half_pow[:], ALU.pow).then_inc(ln_rstd[i], 1)

            def iteration(it, p):
                c = chunks_of(it)
                S, A, M, O = (c.get(x) for x in "SAMO")
                for s in range(SLOTS):
                    if M is not None and s == 0:
                        pool.wait_ge(x2t_hi_done, at(M, 1, 1))
                        pool.wait_ge(x2t_done, at(M, 1, 1))
                        pool.tensor_tensor(x2t_lo[:], x2t[:], x2t_hi[:].bitcast(F32), ALU.subtract)\
                            .then_inc(x2t_lo_done, 1)
                    if S is not None:
                        for h in range(HALVES):
                            u = 2 * s + h
                            if s == 0:
                                pool.wait_ge(gate_step, at(S - 1, 4, 0))
                            else:
                                pool.wait_ge(add_done, at(S, ADDS, u - 3))
                            if h == 0:
                                pool.wait_ge(c_taken, at(S, NSTATE, s + 1))
                            pool.wait_ge(scan_done, at(S, UNITS, u + 1))
                            pool.tensor_tensor(prod[:, h, :] if s else ysum[:, 1 - p, h, :],
                                               state[:, u % SCAN_RING, :], c_all[:, s % C_RING, :], ALU.mult)\
                                .then_inc(prod_done, 1)
                    if O is not None and s == 11:
                        rstd(O, 2)
                    if A is not None and s == 2:
                        rstd(A, 0)
                    if A is not None and s == 15:
                        rstd(A, 1)
                    if S is not None:
                        for h in range(HALVES):
                            y = ysum[:, 1 - p, h, :]
                            if s:
                                pool.wait_ge(prod_done, at(S, UNITS, 2 * s + h + 1))
                                pool.tensor_tensor(y, y, prod[:, h, :], ALU.add).then_inc(add_done, 1)
                    if A is not None and s == 4:
                        pool.wait_ge(a_filled, a_count(A, "x1t"))
                        pool.tensor_tensor(x1[:], x1[:], bo[:].unsqueeze(1).to_broadcast([P, NT, D]),
                                           ALU.add).then_inc(x1_biased, 1)

            run(pool, iteration)


def kernel(**inputs):
    import numpy as np
    import concourse.bacc as bacc
    from concourse.bass_utils import run_bass_kernel_spmd

    a = {k: np.asarray(v) for k, v in inputs.items()}

    def halves(m):
        return m.reshape(HALVES, P, -1).transpose(1, 0, 2).reshape(P, -1)

    params = np.zeros((P, NCOLS), np.float32)

    def put(name, m, row0=0):
        lo = COLS[name][0]
        params[row0:row0 + m.shape[0], lo:lo + m.shape[1]] = m

    rows = np.arange(P)[:, None]
    put("conv_w", halves(a["L0_attn_conv_w"]))
    put("conv_b", halves(a["L0_attn_conv_b"][:, None]))
    put("b_dt", halves(a["L0_attn_b_dt"][:, None]))
    put("skip_d", halves(a["L0_attn_D"][:, None]))
    put("a_log", halves(a["L0_attn_A_log"]))
    put("bq", a["L0_xattn_wq_b"][:, None])
    put("bk", a["L0_xattn_wk_b"][:, None])
    put("bv", a["L0_xattn_wv_b"][:, None])
    put("b1", a["L0_ffn_fc1_b"].reshape(NEXP * HB4, P).T)
    put("router", a["L0_ffn_router_w"].T)
    put("group_mask", (rows // 32 == np.arange(4)).astype(np.float32))
    put("head_mask", (rows // DH % 4 == np.arange(4)).astype(np.float32))
    put("half_mask", (rows // 64 == np.arange(2)).astype(np.float32))
    put("ident", np.eye(P, dtype=np.float32))
    put("bo_row", a["L0_xattn_wo_b"][None])
    put("b2_rows", a["L0_ffn_fc2_b"])
    put("w_dt_rows", a["L0_attn_W_dt"].T, 96)
    put("select", (np.arange(96)[:, None] % 32 == np.arange(32)).astype(np.float32))
    put("tie_order", np.tile(np.arange(NEXP, 0, -1, dtype=np.float32), (P, 1)))
    xp = a["L0_attn_W_xp"].T
    bc, low = xp[:, DTR:], xp[:, :DTR]
    put("w_xp", halves(np.concatenate([bc, bc, bc, low], 1)))
    put("w_in", a["L0_attn_W_in"].T)
    put("w_out", halves(a["L0_attn_W_out"].T))
    for n in "qkvo":
        put(f"w{n}", a[f"L0_xattn_w{n}_w"].T)

    def transposed(x):
        return np.ascontiguousarray(x.reshape(CHUNKS, TOK, D).transpose(0, 2, 1))

    arrays = {
        "x_t": transposed(a["x"]),
        "x_tok": np.ascontiguousarray(a["x"].reshape(CHUNKS, NT, P, D).transpose(0, 2, 1, 3)),
        "ctx_t": transposed(a["ctx_1024"]),
        "params": params,
        "w1": np.ascontiguousarray(a["L0_ffn_fc1_w"].transpose(2, 0, 1).reshape(D, NEXP * HID)),
        "w2": np.ascontiguousarray(
            a["L0_ffn_fc2_w"].reshape(NEXP, D, HB4, P).transpose(3, 0, 2, 1).reshape(P, NEXP * HB4 * D)),
    }
    nc = bacc.Bacc("TRN2", target_bir_lowering=False, num_devices=1)
    args = [nc.dram_tensor(n, v.shape, mybir.dt.from_np(v.dtype), kind="ExternalInput").ap()
            for n, v in arrays.items()]
    out = nc.dram_tensor("out", (CHUNKS, P, NT, D), mybir.dt.float32, kind="ExternalOutput").ap()
    decoder_layer(nc, *args, out)
    r = run_bass_kernel_spmd(nc, [arrays], core_ids=[0])
    y = r.results[0]["out"]
    return np.ascontiguousarray(y.transpose(0, 2, 1, 3)).reshape(BATCH, SEQ, D)
```
